# Optimizing a Trainium2 kernel written in Bass

```python
import numpy as np
import jax
import jax.numpy as jnp

def _softmax(x, axis=-1):
    return jax.nn.softmax(x, axis=axis)

def _gelu(x):
    return jax.nn.gelu(x, approximate=True)

def _silu(x):
    return jax.nn.silu(x)

def _sigmoid(x):
    return jax.nn.sigmoid(x)

def _layernorm(x, axis=-1, eps=1e-05):
    m = jnp.mean(x, axis=axis, keepdims=True)
    v = jnp.var(x, axis=axis, keepdims=True)
    return (x - m) / jnp.sqrt(v + eps)

def _scatter_add(tgt, idx, src, axis=0):
    return tgt.at[idx].add(src)

def _segment_sum(src, seg, n):
    return jax.ops.segment_sum(src, seg, n)
kernel_name = 'mk_seq_postln_d2_jaxref_r8_a5a202'

def setup_inputs(seed: int=0):
    np.random.seed(seed)
    _w = jnp.asarray

    def _L0_attn_setup():
        import jax, jax.numpy as jnp
        import numpy as np
        H = 16
        ROPE_BASE = 10000.0

        def _rotate_half(x):
            d = x.shape[-1]
            return jnp.concatenate((-x[..., d // 2:], x[..., :d // 2]), axis=-1)
        key = jax.random.key(seed)
        ks = jax.random.split(key, 9)
        B, S, E = (4, 256, 128)
        s = 0.02
        return {'x': jax.random.normal(ks[0], (B, S, E), dtype=jnp.float32), 'wq': jax.random.normal(ks[1], (E, E), dtype=jnp.float32) * s, 'bq': jax.random.normal(ks[2], (E,), dtype=jnp.float32) * s, 'wk': jax.random.normal(ks[3], (E, E), dtype=jnp.float32) * s, 'bk': jax.random.normal(ks[4], (E,), dtype=jnp.float32) * s, 'wv': jax.random.normal(ks[5], (E, E), dtype=jnp.float32) * s, 'bv': jax.random.normal(ks[6], (E,), dtype=jnp.float32) * s, 'wo': jax.random.normal(ks[7], (E, E), dtype=jnp.float32) * s, 'bo': jax.random.normal(ks[8], (E,), dtype=jnp.float32) * s}
    _L0_attn_in = _L0_attn_setup()

    def _L0_ffn_setup():
        import jax, jax.numpy as jnp
        import numpy as np
        LN_EPS = 1e-05

        def _swiglu(h, w_gate_up, w_down):
            gu = h @ w_gate_up.T
            gate, up = jnp.split(gu, 2, axis=-1)
            return jax.nn.silu(gate) * up @ w_down.T
        key = jax.random.key(seed)
        ks = jax.random.split(key, 6)
        d_model, d_ff, E = (128, 512, 8)
        shared_d_ff = d_ff // 4
        routed_d_ff = d_ff - shared_d_ff
        B, S = (4, 256)
        x = jax.random.normal(ks[0], (B, S, d_model), dtype=jnp.float32)
        ln_gamma = jnp.ones((d_model,), jnp.float32)
        ln_beta = jnp.zeros((d_model,), jnp.float32)
        router_w = jax.random.normal(ks[1], (E, d_model), jnp.float32) * 0.02
        gate_up_w = jax.random.normal(ks[2], (E, 2 * routed_d_ff, d_model), jnp.float32) * (1.0 / np.sqrt(d_model))
        down_w = jax.random.normal(ks[3], (E, d_model, routed_d_ff), jnp.float32) * (1.0 / np.sqrt(routed_d_ff))
        shared_gate_up_w = jax.random.normal(ks[4], (2 * shared_d_ff, d_model), jnp.float32) * (1.0 / np.sqrt(d_model))
        shared_down_w = jax.random.normal(ks[5], (d_model, shared_d_ff), jnp.float32) * (1.0 / np.sqrt(shared_d_ff))
        return dict(x=x, ln_gamma=ln_gamma, ln_beta=ln_beta, router_w=router_w, gate_up_w=gate_up_w, down_w=down_w, shared_gate_up_w=shared_gate_up_w, shared_down_w=shared_down_w)
    _L0_ffn_in = _L0_ffn_setup()

    def _L1_attn_setup():
        import jax, jax.numpy as jnp
        import numpy as np
        DIM = 128
        DIM_HEAD = 128
        HEADS = 8
        DIM_INNER = DIM_HEAD * HEADS
        key = jax.random.key(seed)
        k_x, k_qkv, k_out = jax.random.split(key, 3)
        x = jax.random.normal(k_x, (2, 256, DIM), dtype=jnp.float32)
        gamma = jnp.ones((DIM,), dtype=jnp.float32)
        w_qkv = jax.random.uniform(k_qkv, (DIM_INNER * 3, DIM), dtype=jnp.float32, minval=-1.0, maxval=1.0) / np.sqrt(DIM)
        w_out = jax.random.uniform(k_out, (DIM, DIM_INNER), dtype=jnp.float32, minval=-1.0, maxval=1.0) / np.sqrt(DIM_INNER)
        return {'x': x, 'gamma': gamma, 'w_qkv': w_qkv, 'w_out': w_out}
    _L1_attn_in = _L1_attn_setup()

    def _L1_ffn_setup():
        import jax, jax.numpy as jnp
        import numpy as np
        EPS = 1e-05

        def _layernorm(x, w, b):
            mu = jnp.mean(x, axis=-1, keepdims=True)
            var = jnp.mean((x - mu) ** 2, axis=-1, keepdims=True)
            return (x - mu) * jax.lax.rsqrt(var + EPS) * w + b

        def _rope_tables(T, D, base=10000.0):
            inv_freq = 1.0 / base ** (jnp.arange(0, D, 2, dtype=jnp.float32) / D)
            t = jnp.arange(T, dtype=jnp.float32)
            freqs = jnp.einsum('i,j->ij', t, inv_freq)
            emb = jnp.concatenate([freqs, freqs], axis=-1)
            return (jnp.cos(emb), jnp.sin(emb))

        def _rotate_half(x):
            x1, x2 = (x[..., :x.shape[-1] // 2], x[..., x.shape[-1] // 2:])
            return jnp.concatenate([-x2, x1], axis=-1)

        def _attn(x, ln_w, ln_b, conv_w, attn_w, proj_w, n_head):
            B, T, C = x.shape
            D = C // n_head
            h = _layernorm(x, ln_w, ln_b)
            hc = jnp.transpose(h, (0, 2, 1))
            hc = jnp.pad(hc, ((0, 0), (0, 0), (2, 0)))
            hc = jax.lax.conv_general_dilated(hc, conv_w, window_strides=(1,), padding='VALID', dimension_numbers=('NCH', 'OIH', 'NCH'), feature_group_count=C)
            h = jnp.transpose(hc, (0, 2, 1))
            qkv = h @ attn_w
            q, k, v = jnp.split(qkv, 3, axis=-1)
            q = q.reshape(B, T, n_head, D)
            k = k.reshape(B, T, n_head, D)
            v = v.reshape(B, T, n_head, D)
            cos, sin = _rope_tables(T, D)
            cos = cos[None, :, None, :]
            sin = sin[None, :, None, :]
            q = q * cos + _rotate_half(q) * sin
            k = k * cos + _rotate_half(k) * sin
            scores = jnp.einsum('bqhd,bkhd->bhqk', q, k) / jnp.sqrt(jnp.float32(D))
            causal = jnp.tril(jnp.ones((T, T), dtype=bool))
            scores = jnp.where(causal, scores, jnp.float32(-1e+30))
            p = jax.nn.softmax(scores, axis=-1)
            y = jnp.einsum('bhqk,bkhd->bqhd', p, v).reshape(B, T, C)
            return y @ proj_w

        def _moe(x, ln_w, ln_b, router_w, expert_wv, expert_proj):
            h = _layernorm(x, ln_w, ln_b)
            logits = h @ router_w
            expert_idx = jnp.argmax(logits, axis=-1)
            E = router_w.shape[-1]
            out = jnp.zeros_like(x)
            for e in range(E):
                gv = h @ expert_wv[e]
                gate_raw, value = jnp.split(gv, 2, axis=-1)
                y = gate_raw * jax.nn.sigmoid(gate_raw) * value @ expert_proj[e]
                out = out + jnp.where((expert_idx == e)[..., None], y, 0.0)
            return out
        C, H, E, B, T = (128, 16, 4, 4, 128)
        Dff = 4 * C
        key = jax.random.key(seed)
        ks = jax.random.split(key, 8)
        s = 0.02
        return {'x': jax.random.normal(ks[0], (B, T, C), dtype=jnp.float32), 'ln1_w': jnp.ones((C,), jnp.float32), 'ln1_b': jnp.zeros((C,), jnp.float32), 'ln2_w': jnp.ones((C,), jnp.float32), 'ln2_b': jnp.zeros((C,), jnp.float32), 'conv_w': jax.random.normal(ks[1], (C, 1, 3), dtype=jnp.float32) * 0.1, 'attn_w': jax.random.normal(ks[2], (C, 3 * C), dtype=jnp.float32) * s, 'proj_w': jax.random.normal(ks[3], (C, C), dtype=jnp.float32) * s, 'router_w': jax.random.normal(ks[4], (C, E), dtype=jnp.float32) * s, 'expert_wv': jax.random.normal(ks[5], (E, C, 2 * Dff), dtype=jnp.float32) * s, 'expert_proj': jax.random.normal(ks[6], (E, Dff, C), dtype=jnp.float32) * s}
    _L1_ffn_in = _L1_ffn_setup()
    _d = {'L0_attn_x': _L0_attn_in['x'], 'L0_attn_wq': _L0_attn_in['wq'], 'L0_attn_bq': _L0_attn_in['bq'], 'L0_attn_wk': _L0_attn_in['wk'], 'L0_attn_bk': _L0_attn_in['bk'], 'L0_attn_wv': _L0_attn_in['wv'], 'L0_attn_bv': _L0_attn_in['bv'], 'L0_attn_wo': _L0_attn_in['wo'], 'L0_attn_bo': _L0_attn_in['bo'], 'L0_ffn_ln_gamma': _L0_ffn_in['ln_gamma'], 'L0_ffn_ln_beta': _L0_ffn_in['ln_beta'], 'L0_ffn_router_w': _L0_ffn_in['router_w'], 'L0_ffn_gate_up_w': _L0_ffn_in['gate_up_w'], 'L0_ffn_down_w': _L0_ffn_in['down_w'], 'L0_ffn_shared_gate_up_w': _L0_ffn_in['shared_gate_up_w'], 'L0_ffn_shared_down_w': _L0_ffn_in['shared_down_w'], 'L1_attn_gamma': _L1_attn_in['gamma'], 'L1_attn_w_qkv': _L1_attn_in['w_qkv'], 'L1_attn_w_out': _L1_attn_in['w_out'], 'L1_ffn_ln1_w': _L1_ffn_in['ln1_w'], 'L1_ffn_ln1_b': _L1_ffn_in['ln1_b'], 'L1_ffn_ln2_w': _L1_ffn_in['ln2_w'], 'L1_ffn_ln2_b': _L1_ffn_in['ln2_b'], 'L1_ffn_conv_w': _L1_ffn_in['conv_w'], 'L1_ffn_attn_w': _L1_ffn_in['attn_w'], 'L1_ffn_proj_w': _L1_ffn_in['proj_w'], 'L1_ffn_router_w': _L1_ffn_in['router_w'], 'L1_ffn_expert_wv': _L1_ffn_in['expert_wv'], 'L1_ffn_expert_proj': _L1_ffn_in['expert_proj']}
    _x0 = _d['L0_attn_x']
    _d['L0_attn_x'] = jax.random.normal(jax.random.fold_in(jax.random.key(seed), 1), (1, 2048, 128), dtype=_x0.dtype)
    del _x0
    return _d

def reference(L0_attn_x, L0_attn_wq, L0_attn_bq, L0_attn_wk, L0_attn_bk, L0_attn_wv, L0_attn_bv, L0_attn_wo, L0_attn_bo, L0_ffn_ln_gamma, L0_ffn_ln_beta, L0_ffn_router_w, L0_ffn_gate_up_w, L0_ffn_down_w, L0_ffn_shared_gate_up_w, L0_ffn_shared_down_w, L1_attn_gamma, L1_attn_w_qkv, L1_attn_w_out, L1_ffn_ln1_w, L1_ffn_ln1_b, L1_ffn_ln2_w, L1_ffn_ln2_b, L1_ffn_conv_w, L1_ffn_attn_w, L1_ffn_proj_w, L1_ffn_router_w, L1_ffn_expert_wv, L1_ffn_expert_proj):

    def _L0_attn_ref(x, wq, bq, wk, bk, wv, bv, wo, bo):
        import jax, jax.numpy as jnp
        import numpy as np
        H = 16
        ROPE_BASE = 10000.0

        def _rotate_half(x):
            d = x.shape[-1]
            return jnp.concatenate((-x[..., d // 2:], x[..., :d // 2]), axis=-1)
        B, S, E = x.shape
        D = E // H

        def proj(w, b):
            return (x @ w.T + b).reshape(B, S, H, D).transpose(0, 2, 1, 3)
        q = proj(wq, bq)
        k = proj(wk, bk)
        v = proj(wv, bv)
        inv_freq = 1.0 / ROPE_BASE ** (jnp.arange(0, D, 2, dtype=jnp.float32) / D)
        freqs = jnp.arange(S, dtype=jnp.float32)[:, None] * inv_freq[None, :]
        cos = jnp.repeat(jnp.cos(freqs), 2, axis=-1)[None, None]
        sin = jnp.repeat(jnp.sin(freqs), 2, axis=-1)[None, None]
        q = q * cos + _rotate_half(q) * sin
        k = k * cos + _rotate_half(k) * sin
        scale = D ** (-0.5)
        scores = jnp.einsum('bhqd,bhkd->bhqk', q, k) * scale
        attn = jax.nn.softmax(scores, axis=-1)
        out = jnp.einsum('bhqk,bhkd->bhqd', attn, v)
        out = out.transpose(0, 2, 1, 3).reshape(B, S, E)
        return out @ wo.T + bo

    def _L0_ffn_ref(x, ln_gamma, ln_beta, router_w, gate_up_w, down_w, shared_gate_up_w, shared_down_w):
        import jax, jax.numpy as jnp
        import numpy as np
        LN_EPS = 1e-05

        def _swiglu(h, w_gate_up, w_down):
            gu = h @ w_gate_up.T
            gate, up = jnp.split(gu, 2, axis=-1)
            return jax.nn.silu(gate) * up @ w_down.T
        B, S, D = x.shape
        E = router_w.shape[0]
        top_k = 2
        xt = x.reshape(-1, D)
        mu = jnp.mean(xt, axis=-1, keepdims=True)
        var = jnp.mean(jnp.square(xt - mu), axis=-1, keepdims=True)
        normed = (xt - mu) * jax.lax.rsqrt(var + LN_EPS) * ln_gamma + ln_beta
        logits = normed.astype(jnp.float32) @ router_w.T
        probs = jax.nn.softmax(logits, axis=-1)
        top_v, top_i = jax.lax.top_k(probs, top_k)
        gates = jax.nn.softmax(top_v, axis=-1)
        comb = jnp.sum(jax.nn.one_hot(top_i, E, dtype=gates.dtype) * gates[..., None], axis=1)
        out = jnp.zeros_like(normed)
        for e in range(E):
            y = _swiglu(normed, gate_up_w[e], down_w[e])
            out = out + comb[:, e, None] * y
        out = out + _swiglu(normed, shared_gate_up_w, shared_down_w)
        return out.reshape(B, S, D)

    def _L1_attn_ref(x, gamma, w_qkv, w_out):
        import jax, jax.numpy as jnp
        import numpy as np
        DIM = 128
        DIM_HEAD = 128
        HEADS = 8
        DIM_INNER = DIM_HEAD * HEADS
        scale_norm = DIM ** 0.5
        scale_attn = DIM_HEAD ** (-0.5)
        l2 = jnp.sqrt(jnp.sum(x * x, axis=-1, keepdims=True))
        xn = x / jnp.maximum(l2, 1e-12) * scale_norm * gamma
        qkv = jnp.einsum('bnc,fc->bnf', xn, w_qkv)
        b, n, _ = qkv.shape
        qkv = qkv.reshape(b, n, 3, HEADS, DIM_HEAD)
        q, k, v = (qkv[:, :, 0], qkv[:, :, 1], qkv[:, :, 2])
        q = q * scale_attn
        sim = jnp.einsum('bihd,bjhd->bhij', q, k)
        causal_mask = jnp.triu(jnp.ones((n, n), dtype=bool), k=1)
        neg = -jnp.finfo(sim.dtype).max
        sim = jnp.where(causal_mask, neg, sim)
        attn = jax.nn.softmax(sim, axis=-1)
        out = jnp.einsum('bhij,bjhd->bihd', attn, v)
        out = out.reshape(b, n, DIM_INNER)
        return jnp.einsum('bnf,cf->bnc', out, w_out)

    def _L1_ffn_ref(x, ln1_w, ln1_b, ln2_w, ln2_b, conv_w, attn_w, proj_w, router_w, expert_wv, expert_proj):
        import jax, jax.numpy as jnp
        import numpy as np
        EPS = 1e-05

        def _layernorm(x, w, b):
            mu = jnp.mean(x, axis=-1, keepdims=True)
            var = jnp.mean((x - mu) ** 2, axis=-1, keepdims=True)
            return (x - mu) * jax.lax.rsqrt(var + EPS) * w + b

        def _rope_tables(T, D, base=10000.0):
            inv_freq = 1.0 / base ** (jnp.arange(0, D, 2, dtype=jnp.float32) / D)
            t = jnp.arange(T, dtype=jnp.float32)
            freqs = jnp.einsum('i,j->ij', t, inv_freq)
            emb = jnp.concatenate([freqs, freqs], axis=-1)
            return (jnp.cos(emb), jnp.sin(emb))

        def _rotate_half(x):
            x1, x2 = (x[..., :x.shape[-1] // 2], x[..., x.shape[-1] // 2:])
            return jnp.concatenate([-x2, x1], axis=-1)

        def _attn(x, ln_w, ln_b, conv_w, attn_w, proj_w, n_head):
            B, T, C = x.shape
            D = C // n_head
            h = _layernorm(x, ln_w, ln_b)
            hc = jnp.transpose(h, (0, 2, 1))
            hc = jnp.pad(hc, ((0, 0), (0, 0), (2, 0)))
            hc = jax.lax.conv_general_dilated(hc, conv_w, window_strides=(1,), padding='VALID', dimension_numbers=('NCH', 'OIH', 'NCH'), feature_group_count=C)
            h = jnp.transpose(hc, (0, 2, 1))
            qkv = h @ attn_w
            q, k, v = jnp.split(qkv, 3, axis=-1)
            q = q.reshape(B, T, n_head, D)
            k = k.reshape(B, T, n_head, D)
            v = v.reshape(B, T, n_head, D)
            cos, sin = _rope_tables(T, D)
            cos = cos[None, :, None, :]
            sin = sin[None, :, None, :]
            q = q * cos + _rotate_half(q) * sin
            k = k * cos + _rotate_half(k) * sin
            scores = jnp.einsum('bqhd,bkhd->bhqk', q, k) / jnp.sqrt(jnp.float32(D))
            causal = jnp.tril(jnp.ones((T, T), dtype=bool))
            scores = jnp.where(causal, scores, jnp.float32(-1e+30))
            p = jax.nn.softmax(scores, axis=-1)
            y = jnp.einsum('bhqk,bkhd->bqhd', p, v).reshape(B, T, C)
            return y @ proj_w

        def _moe(x, ln_w, ln_b, router_w, expert_wv, expert_proj):
            h = _layernorm(x, ln_w, ln_b)
            logits = h @ router_w
            expert_idx = jnp.argmax(logits, axis=-1)
            E = router_w.shape[-1]
            out = jnp.zeros_like(x)
            for e in range(E):
                gv = h @ expert_wv[e]
                gate_raw, value = jnp.split(gv, 2, axis=-1)
                y = gate_raw * jax.nn.sigmoid(gate_raw) * value @ expert_proj[e]
                out = out + jnp.where((expert_idx == e)[..., None], y, 0.0)
            return out
        n_head = 16
        x = x + _attn(x, ln1_w, ln1_b, conv_w, attn_w, proj_w, n_head)
        x = x + _moe(x, ln2_w, ln2_b, router_w, expert_wv, expert_proj)
        return x
    x = L0_attn_x
    x = _layernorm(x + _L0_attn_ref(x, L0_attn_wq, L0_attn_bq, L0_attn_wk, L0_attn_bk, L0_attn_wv, L0_attn_bv, L0_attn_wo, L0_attn_bo), axis=-1)
    x = _layernorm(x + _L0_ffn_ref(x, L0_ffn_ln_gamma, L0_ffn_ln_beta, L0_ffn_router_w, L0_ffn_gate_up_w, L0_ffn_down_w, L0_ffn_shared_gate_up_w, L0_ffn_shared_down_w), axis=-1)
    x = _layernorm(x + _L1_attn_ref(x, L1_attn_gamma, L1_attn_w_qkv, L1_attn_w_out), axis=-1)
    x = _layernorm(x + _L1_ffn_ref(x, L1_ffn_ln1_w, L1_ffn_ln1_b, L1_ffn_ln2_w, L1_ffn_ln2_b, L1_ffn_conv_w, L1_ffn_attn_w, L1_ffn_proj_w, L1_ffn_router_w, L1_ffn_expert_wv, L1_ffn_expert_proj), axis=-1)
    return x

_drawn_inputs = setup_inputs


def setup_inputs(seed=0):
    import zlib

    import numpy as np

    out = dict(_drawn_inputs(seed))
    spreads = {'L0_ffn_ln_gamma': (1.0, 0.2),
     'L0_ffn_ln_beta': (0.0, 0.1),
     'L1_attn_gamma': (1.0, 0.6),
     'L1_ffn_ln1_w': (1.0, 0.6),
     'L1_ffn_ln1_b': (0.0, 0.8),
     'L1_ffn_ln2_w': (1.0, 0.6),
     'L1_ffn_ln2_b': (0.0, 0.8)}
    factors = {'L0_attn_wq': 8.0,
     'L0_attn_bq': 8.0,
     'L0_attn_wk': 8.0,
     'L0_attn_bk': 8.0,
     'L0_attn_wv': 8.0,
     'L0_attn_bv': 2.83,
     'L1_ffn_conv_w': 8.0,
     'L1_ffn_attn_w': 8.0,
     'L1_ffn_proj_w': 8.0,
     'L1_ffn_router_w': 8.0,
     'L1_ffn_expert_wv': 8.0,
     'L1_ffn_expert_proj': 8.0}
    for name, (base, spread) in spreads.items():
        noise = np.random.default_rng([zlib.crc32(name.encode()), seed]).standard_normal(out[name].shape)
        drawn = base * np.exp(spread * noise) if base else spread * noise
        out[name] = jnp.asarray(drawn.astype(out[name].dtype))
    for name, factor in factors.items():
        out[name] = (out[name] * factor).astype(out[name].dtype)
    return out
```

```python
from contextlib import ExitStack

import concourse.bass as bass
from concourse import mybir

F32 = mybir.dt.float32
BF16 = mybir.dt.bfloat16
ALU = mybir.AluOpType
ACT = mybir.ActivationFunctionType
AX = mybir.AxisListType

P = 128
T = 2048
NT = T // P
BLK = 512
NB = T // BLK
TPB = BLK // P
HEADS, HD = 16, 8
NPACK = 4
HPP = HEADS // NPACK
TERMS = 3
PROD = TERMS * TERMS * HD
SHIFT0 = PROD
ROWS = PROD + TERMS
LN_EPS = 1e-5
BIG_HEADS, BIG_HD = 8, 128
NEG = -3.0e38
START = 1


def is_first(block):
    return isinstance(block, int) and block == 0


class Core:

    def __init__(self, nc, stack):
        self.nc, self.used = nc, []
        self.psum = stack.enter_context(nc.psum_tensor("psum", [P, 8, BLK], F32))

    def sb(self, stack, name, shape, dt=F32):
        return stack.enter_context(self.nc.sbuf_tensor(name, shape, dt))

    def sem(self, stack, name):
        self.used.append(self.nc.alloc_semaphore(name))
        return self.used[-1]

    def recycle_semaphores(self):
        self.nc.clear_and_free_semaphores(self.used)
        self.nc.all_engine_barrier()
        self.used = []


def start_counts(eng, *sems):
    for s in sems:
        eng.sem_inc(s, START)


class Chain:

    def __init__(self, eng, sem):
        self.eng, self.sem, self.n = eng, sem, 0

    def link(self, ins):
        self.n += 1
        ins.then_inc(self.sem, 1)

    def settle(self):
        self.eng.wait_ge(self.sem, self.n)


def layer_norm(eng, chain, x, out, st, var_ready, rstd_ready, tiles):
    stats, mv, veps, rstd = st
    for t in tiles:
        chain.link(eng.bn_stats(stats[:, t, :], x[:, t, :]))
    chain.settle()
    for t in tiles:
        chain.link(eng.bn_aggr(mv[:, t, :], stats[:, t, :]))
    chain.settle()
    eng.tensor_scalar(veps[:, :], mv[:, :, 1], LN_EPS, None, ALU.add).then_inc(var_ready[0], 1)
    eng.wait_ge(rstd_ready[0], rstd_ready[1])
    for t in tiles:
        chain.link(eng.tensor_scalar(out[:, t, :], x[:, t, :], mv[:, t, 0:1], rstd[:, t:t + 1],
                                     ALU.subtract, ALU.mult))
    chain.settle()


def rsqrt_pool(eng, st, half, var_ready, rstd_ready, n):
    eng.wait_ge(var_ready, n)
    eng.tensor_tensor(st[3][:, :], st[2][:, :], half[:, :], ALU.pow).then_inc(rstd_ready, 1)


def small_head_projections(core, tag, src_T, dram, KS, QS, V, biased, table, scratch):
    nc, ps = core.nc, core.psum
    with ExitStack() as st:
        sem = lambda n: core.sem(st, f"{tag}_{n}")
        sb = lambda n, s, dt=F32: core.sb(st, f"{tag}_{n}", s, dt)
        w = {n: sb(n, [P, P]) for n in ("wq", "wqr", "wk", "wkr", "wv")}
        b = {n: sb(n, [P, 1]) for n in ("bq", "bqr", "bk", "bkr")} if biased else {}
        bv = sb("bv", [P, P]) if biased else None
        cs = sb("cs", [P, 2, 2, BLK])
        t1, t2 = sb("t1", [P, 2, BLK]), sb("t2", [P, 2, BLK])
        terms = sb("terms", [P, 2, TERMS, BLK], BF16)
        w_in, cs_in = sem("w_in"), [sem("cs_in0"), sem("cs_in1")]
        qk_ready, qk_read = sem("qk_ready"), sem("qk_read")
        v_ready, v_read = sem("v_ready"), sem("v_read")
        rot, hi, rest, mid, low = (sem(n) for n in ("rot", "hi", "rest", "mid", "low"))
        half_done, ones_set = sem("half_done"), sem("ones_set")
        stored, stacked = sem("stored"), [sem("stacked0"), sem("stacked1")]
        steps = [("k", n) for n in range(NB)] + [("q", n) for n in range(NB)]
        NS = len(steps)
        STACKS = 16 * TERMS * TERMS
        with nc.Block() as block:
            @block.sync
            def _(sp):
                for n in w:
                    sp.dma_start(w[n][:, :], dram[n]).then_inc(w_in, 16)
                for n in b:
                    sp.dma_start(b[n][:, :], dram[n]).then_inc(w_in, 16)
                if biased:
                    sp.dma_start(bv[:, :], dram["bv"]).then_inc(w_in, 16)

                def stack_terms(s):
                    which, n = steps[s]
                    sp.wait_ge(stored, 16 * (s + 1))
                    dst = QS if which == "q" else KS
                    for t in range(TERMS):
                        src = scratch[s % 2, t].rearrange("(h d) n -> d h n", d=HD)
                        for r in range(TERMS):
                            row = HD * (TERMS * t + r if which == "q" else TERMS * r + t)
                            sp.dma_start(dst[row:row + HD, :, n * BLK:(n + 1) * BLK], src).then_inc(stacked[s % 2], 16)

                for s, (which, n) in enumerate(steps):
                    if s >= 2:
                        sp.wait_ge(rot, s - 1)
                    sp.dma_start(cs[:, s % 2, :, :], table[:, :, n * BLK:(n + 1) * BLK]).then_inc(cs_in[s % 2], 16)
                    if s >= 1:
                        if s >= 3:
                            sp.wait_ge(stacked[(s - 1) % 2], STACKS * ((s - 1) // 2))
                        sp.wait_ge(low, s)
                        sp.dma_start(scratch[(s - 1) % 2].rearrange("t p n -> p t n"),
                                     terms[:, (s - 1) % 2, :, :]).then_inc(stored, 16)
                        if s == 1:
                            sp.wait_ge(half_done, 2)
                        stack_terms(s - 1)
                sp.wait_ge(low, NS)
                sp.wait_ge(stacked[(NS - 1) % 2], STACKS * ((NS - 1) // 2))
                sp.dma_start(scratch[(NS - 1) % 2].rearrange("t p n -> p t n"),
                             terms[:, (NS - 1) % 2, :, :]).then_inc(stored, 16)
                stack_terms(NS - 1)
                for done in stacked:
                    sp.wait_ge(done, STACKS * (NS // 2))

            @block.gpsimd
            def _(pool):
                pool.memset(KS[64:ROWS, 0:HEADS // 2, :], -1.0).then_inc(half_done, 1)
                pool.wait_ge(half_done, 1)
                pool.memset(KS[64:ROWS, HEADS // 2:, :], -1.0).then_inc(half_done, 1)
                pool.wait_ge(half_done, 2)
                pool.memset(V[:, :, :, HD:], 1.0).then_inc(ones_set, 1)

            @block.tensor
            def _(pe):
                pe.wait_ge(w_in, 16 * (len(w) + len(b) + bool(biased)))
                for s, (which, n) in enumerate(steps):
                    if s >= 2:
                        pe.wait_ge(qk_read, s - 1)
                    cols = src_T[:, n * BLK:(n + 1) * BLK]
                    pe.matmul(ps[:, 2 * (s % 2), :], w["w" + which][:, :], cols, start=True, stop=True)
                    pe.matmul(ps[:, 2 * (s % 2) + 1, :], w["w" + which + "r"][:, :], cols,
                              start=True, stop=True).then_inc(qk_ready, 1)
                for g in range(NB):
                    if g >= 2:
                        pe.wait_ge(v_read, TPB * (g - 1))
                    for i in range(TPB):
                        t = g * TPB + i
                        mm = pe.matmul(ps[:, 4 + g % 2, i * P:(i + 1) * P], src_T[:, t * P:(t + 1) * P],
                                       w["wv"][:, :], start=True, stop=True)
                    mm.then_inc(v_ready, 1)

            @block.scalar
            def _(act):
                for s in range(NS):
                    act.wait_ge(rot, s + 1)
                    if s >= 2:
                        act.wait_ge(stored, 16 * (s - 1))
                    act.activation(terms[:, s % 2, 0, :], t1[:, s % 2, :], ACT.Copy).then_inc(hi, 1)
                    act.wait_ge(rest, s + 1)
                    act.activation(terms[:, s % 2, 1, :], t2[:, s % 2, :], ACT.Copy).then_inc(mid, 1)

            @block.vector
            def _(dve):
                part = Chain(dve, sem("part"))
                dve.wait_ge(w_in, 16 * (len(w) + len(b) + bool(biased)))

                def split(s):
                    u = s % 2
                    dve.wait_ge(hi, s + 1)
                    dve.tensor_tensor(t2[:, u, :], t1[:, u, :], terms[:, u, 0, :], ALU.subtract).then_inc(rest, 1)
                    dve.wait_ge(mid, s + 1)
                    dve.tensor_tensor(terms[:, u, 2, :], t2[:, u, :], terms[:, u, 1, :],
                                      ALU.subtract).then_inc(low, 1)

                for s, (which, n) in enumerate(steps):
                    u = s % 2
                    dve.wait_ge(cs_in[u], 16 * (s // 2 + 1))
                    dve.wait_ge(qk_ready, s + 1)
                    if s >= 2:
                        dve.wait_ge(low, s - 1)
                    for j, (t, name) in enumerate(((t1, "b" + which), (t2, "b" + which + "r"))):
                        src = ps[:, 2 * u + j, :]
                        if biased:
                            ins = dve.scalar_tensor_tensor(out=t[:, u, :], in0=src, scalar=b[name][:, 0:1],
                                                           in1=cs[:, u, j, :], op0=ALU.add, op1=ALU.mult)
                        else:
                            ins = dve.tensor_tensor(t[:, u, :], src, cs[:, u, j, :], ALU.mult)
                        part.link(ins)
                    part.settle()
                    dve.tensor_tensor(t1[:, u, :], t1[:, u, :], t2[:, u, :], ALU.add).then_inc(rot, 1)
                    dve.sem_inc(qk_read, 1)
                    if s >= 1:
                        split(s - 1)
                split(NS - 1)
                dve.wait_ge(ones_set, 1)
                for t in range(NT):
                    g, i = t // TPB, t % TPB
                    dve.wait_ge(v_ready, g + 1)
                    src = ps[:, 4 + g % 2, i * P:(i + 1) * P].rearrange("p (h d) -> p h d", d=HD)
                    if biased:
                        ins = dve.tensor_tensor(V[:, t, :, 0:HD], src,
                                                bv[:, :].rearrange("p (h d) -> p h d", d=HD), ALU.add)
                    else:
                        ins = dve.tensor_copy(V[:, t, :, 0:HD], src)
                    ins.then_inc(v_read, 1)


MAX_W = 2 * BLK
S_BANK, S_SLOTS = 4, 3
AV_BANK = 7
P_SLOTS = 8


def small_head_attention(core, tag, KS, QS, V, OT, sel, diag_neg, causal):
    nc, ps = core.nc, core.psum
    scale = float(HD) ** -0.5

    def key_tiles(qb):
        return TPB * (qb + 1) if causal else NT

    def units(qb):
        out = []
        for p in range(NPACK):
            mine = []
            for j in range(HPP):
                for qt in range(TPB):
                    keys = (TPB * qb + qt + 1) * P if causal else T
                    for u in range(-(-keys // MAX_W)):
                        mine.append(("scores", p, j, qt, u, min(MAX_W, keys - u * MAX_W)))
            out.append(mine)
        return out

    def items(qb):
        us = units(qb)
        row = list(us[0])
        for p in range(1, NPACK):
            row += us[p][:2] + [("turn", p - 1)] + us[p][2:]
        return row + [("turn", NPACK - 1)]

    def parts(qb):
        return -(-((TPB * (qb + 1)) * P if causal else T) // MAX_W)

    n_items = [len(items(q)) for q in range(NB)]
    n_exp = [HEADS * key_tiles(q) for q in range(NB)]
    n_step = [NPACK * key_tiles(q) for q in range(NB)]

    def before(counts, qb):
        return sum(counts[:qb]) if isinstance(qb, int) else qb * counts[0]

    with ExitStack() as st:
        sem = lambda n: core.sem(st, f"{tag}_{n}")
        sb = lambda n, s, dt=F32: core.sb(st, f"{tag}_{n}", s, dt)
        probs = sb("probs", [P, P_SLOTS, BLK])
        OD = sb("OD", [P, NPACK, BLK])
        rden = sb("rden", [P, BLK])
        mx = sb("mx", [P, 2, TPB, HPP, 2])
        mxr = sb("mxr", [P, 2, TPB, HPP])
        mrow = sb("mrow", [HPP, 2, BLK])
        mrest = sb("mrest", [HPP, BLK])
        zero4 = sb("zero4", [HPP, BLK])
        mterm = sb("mterm", [HPP, 2, TERMS, BLK], BF16)
        bank_zeroed, zero_set = sem("bank_zeroed"), sem("zero_set")
        max_ready, max_read, mx_ready = sem("max_ready"), sem("max_read"), sem("mx_ready")
        masked_neg, row_ready = sem("masked_neg"), sem("row_ready")
        split_step, split_done, shift_in = sem("split_step"), sem("split_done"), [sem(f"shift_in{p}") for p in range(NPACK)]
        s_ready, exp_done, masked, av_done = sem("s_ready"), sem("exp_done"), sem("masked"), sem("av_done")
        od_done, sel_ready, sel_rden, sel_read = sem("od_done"), sem("sel_ready"), sem("sel_rden"), sem("sel_read")

        def q_cols(qb, a, n):
            return slice(qb * BLK + a, qb * BLK + a + n) if isinstance(qb, int) else bass.ds(qb * BLK + a, n)

        def first_col(qb, kt):
            return P * max(0, kt - TPB * qb) if causal else 0

        def blocks(eng, body):
            body(None, 0)
            if causal:
                for qb in range(NB - 1):
                    body(qb, qb + 1)
            else:
                with eng.Fori(0, NB - 1) as qb:
                    body(qb, qb + 1)
            body(NB - 1, None)

        def shape_of(qb):
            return qb if isinstance(qb, int) else 0

        with nc.Block() as block:
            @block.sync
            def _(sp):
                def body(qb, nxt):
                    if nxt is None:
                        return
                    for p in range(NPACK):
                        sp.wait_ge(split_done, NPACK * nxt + p + 1)
                        for j in range(HPP):
                            sp.dma_start(QS[SHIFT0:ROWS, HPP * p + j, q_cols(nxt, 0, BLK)],
                                         mterm[j:j + 1, p % 2, :, :]).then_inc(shift_in[p], 16)
                blocks(sp, body)
                for p in range(NPACK):
                    sp.wait_ge(shift_in[p], 16 * HPP * NB)

            @block.gpsimd
            def _(pool):
                pool.memset(zero4[:, :], 0.0).then_inc(zero_set, 1)
                pool.wait_ge(zero_set, 1)

                def split(nxt, p):
                    n = NPACK * nxt + p
                    u = p % 2
                    if p >= 2:
                        pool.wait_ge(shift_in[p - 2], 16 * HPP * (nxt + 1))
                    elif not is_first(nxt):
                        pool.wait_ge(shift_in[p + 2], 16 * HPP * nxt)
                    pool.wait_ge(row_ready, n + 1)
                    pool.tensor_tensor(mterm[:, u, 0, :], mrow[:, u, :], zero4[:, :], ALU.add).then_inc(split_step, 1)
                    pool.wait_ge(split_step, 3 * n + 1)
                    pool.tensor_tensor(mrest[:, :], mrow[:, u, :], mterm[:, u, 0, :], ALU.subtract).then_inc(split_step, 1)
                    pool.wait_ge(split_step, 3 * n + 2)
                    pool.tensor_tensor(mterm[:, u, 1, :], mrest[:, :], zero4[:, :], ALU.add).then_inc(split_step, 1)
                    pool.wait_ge(split_step, 3 * n + 3)
                    pool.tensor_tensor(mterm[:, u, 2, :], mrest[:, :], mterm[:, u, 1, :],
                                       ALU.subtract).then_inc(split_done, 1)

                def body(qb, nxt):
                    for p in range(NPACK):
                        if qb is not None and causal:
                            for kt in range(TPB * qb, TPB * (qb + 1)):
                                for j in range(HPP):
                                    e = HPP * (p * key_tiles(qb) + kt) + j
                                    c = first_col(qb, kt)
                                    tile = probs[:, e % P_SLOTS, c:c + P]
                                    pool.wait_ge(exp_done, START + before(n_exp, qb) + e + 1)
                                    pool.affine_select(out=tile, in_=tile, compare_op=ALU.is_ge, fill=0.0,
                                                       base=0, pattern=[[1, P]],
                                                       channel_multiplier=-1).then_inc(masked, 1)
                        if nxt is not None and p >= 1:
                            split(nxt, p - 1)
                    if nxt is not None:
                        split(nxt, NPACK - 1)
                blocks(pool, body)

            @block.tensor
            def _(pe):
                start_counts(pe, av_done, sel_ready)
                pe.wait_ge(bank_zeroed, 1)

                def max_item(nxt, k, item):
                    n = before(n_items, nxt) + k
                    slot = k % 2
                    if not is_first(nxt) or k >= 2:
                        pe.wait_ge(max_read, n - 1)
                    if item[0] == "turn":
                        p = item[1]
                        pe.wait_ge(mx_ready, NPACK * nxt + p + 1)
                        for qt in range(TPB):
                            mm = pe.transpose(ps[0:HPP, 2 * slot, qt * P:(qt + 1) * P], mxr[:, p % 2, qt, :],
                                              core.ident[:, :])
                        mm.then_inc(max_ready, 1)
                        return
                    _, p, j, qt, u, width = item
                    h = HPP * p + j
                    for a in range(0, width, BLK):
                        w = min(BLK, width - a)
                        k0 = u * MAX_W + a
                        mm = pe.matmul(ps[:, 2 * slot + a // BLK, 0:w], QS[0:PROD, h, q_cols(nxt, qt * P, P)],
                                       KS[0:PROD, h, k0:k0 + w], start=True, stop=True)
                    mm.then_inc(max_ready, 1)

                def body(qb, nxt):
                    row = items(shape_of(nxt)) if nxt is not None else []
                    if qb is None:
                        for k, item in enumerate(row):
                            max_item(nxt, k, item)
                        return
                    K = key_tiles(shape_of(qb))
                    steps = NPACK * K
                    early = max(len(row) - 1, 0)
                    e0, s0 = before(n_exp, qb), before(n_step, qb)
                    m0 = before([TPB * HEADS] * NB, qb)
                    done = 0

                    def av(s):
                        p, kt = s // K, s % K
                        c = first_col(qb, kt)
                        if kt == 0:
                            pe.wait_ge(od_done, START + NPACK * qb + p)
                        if causal and kt >= TPB * qb:
                            pe.wait_ge(masked, m0 + HPP * (p * TPB + kt - TPB * qb) + HPP)
                        else:
                            pe.wait_ge(exp_done, START + e0 + HPP * s + HPP)
                        for j in range(HPP):
                            e = HPP * s + j
                            mm = pe.matmul(ps[32 * j:32 * j + 2 * HD, AV_BANK, c:BLK], V[:, kt, HPP * p + j, :],
                                           probs[:, e % P_SLOTS, c:BLK], start=(kt == 0), stop=(kt == K - 1),
                                           skip_group_check=True)
                        mm.then_inc(av_done, 1)

                    for s in range(steps):
                        p, kt = s // K, s % K
                        c = first_col(qb, kt)
                        for j in range(HPP):
                            e = HPP * s + j
                            if kt == 0 and j == 0:
                                pe.wait_ge(shift_in[p], 16 * HPP * (qb + 1))
                            if e == 0:
                                pe.wait_ge(sel_read, START + qb)
                            pe.wait_ge(exp_done, START + e0 + max(e - S_SLOTS + 1, 0))
                            h = HPP * p + j
                            pe.matmul(ps[:, S_BANK + e % S_SLOTS, c:BLK], KS[0:ROWS, h, kt * P:(kt + 1) * P],
                                      QS[0:ROWS, h, q_cols(qb, c, BLK - c)], start=True, stop=True).then_inc(s_ready, 1)
                            if j % 2:
                                upto = early * (2 * s + 1 + j // 2) // (2 * steps)
                                while done < upto:
                                    max_item(nxt, done, row[done])
                                    done += 1
                        if s >= 1:
                            av(s - 1)
                    av(steps - 1)
                    if row:
                        max_item(nxt, len(row) - 1, row[-1])
                    pe.wait_ge(od_done, START + NPACK * qb + NPACK)
                    for which in range(2):
                        for p in range(NPACK):
                            mm = pe.matmul(ps[:, S_BANK + which, :], sel[:, which, p, :], OD[:, p, :],
                                           start=(p == 0), stop=(p == NPACK - 1))
                    mm.then_inc(sel_ready, 1)
                blocks(pe, body)

            @block.scalar
            def _(act):
                start_counts(act, exp_done, od_done)

                def body(qb, nxt):
                    if qb is None:
                        return
                    K = key_tiles(shape_of(qb))
                    steps = NPACK * K
                    e0, s0 = before(n_exp, qb), before(n_step, qb)

                    def od_copy(p):
                        act.wait_ge(av_done, START + s0 + K * (p + 1))
                        if p == 0:
                            act.wait_ge(sel_ready, START + qb)
                        act.activation(OD[:, p, :], ps[:, AV_BANK, :], ACT.Copy).then_inc(od_done, 1)

                    for s in range(steps):
                        p, kt = s // K, s % K
                        c = first_col(qb, kt)
                        for j in range(HPP):
                            e = HPP * s + j
                            act.wait_ge(s_ready, e0 + e + 1)
                            if j == 0:
                                act.wait_ge(av_done, START + s0 + max(s - 1, 0))
                            act.activation(probs[:, e % P_SLOTS, c:BLK], ps[:, S_BANK + e % S_SLOTS, c:BLK],
                                           ACT.Exp, scale=scale).then_inc(exp_done, 1)
                        if kt == 0 and p >= 1:
                            od_copy(p - 1)
                    od_copy(NPACK - 1)
                blocks(act, body)

            @block.vector
            def _(dve):
                start_counts(dve, sel_read)
                dve.memset(ps[:, AV_BANK, :], 0.0).then_inc(bank_zeroed, 1)

                def max_item(nxt, k, item, neg):
                    n = before(n_items, nxt) + k
                    slot = k % 2
                    dve.wait_ge(max_ready, n + 1)
                    if item[0] == "turn":
                        p = item[1]
                        r = NPACK * nxt + p
                        if not is_first(nxt) or p >= 2:
                            dve.wait_ge(split_done, r - 1)
                        dve.tensor_copy(mrow[:, p % 2, :], ps[0:HPP, 2 * slot, :]).then_inc(row_ready, 1)
                        dve.wait_ge(row_ready, r + 1)
                        dve.sem_inc(max_read, 1)
                        return neg
                    _, p, j, qt, u, width = item
                    banks = ps[:, 2 * slot:2 * slot + 2, :].rearrange("p b n -> p (b n)")
                    if causal and u == parts(nxt) - 1:
                        diag = banks[:, width - P:width]
                        neg += 1
                        dve.tensor_tensor(diag, diag, diag_neg[:, :], ALU.add).then_inc(masked_neg, 1)
                        dve.wait_ge(masked_neg, neg)
                    dve.tensor_reduce(mx[:, p % 2, qt, j, u:u + 1], banks[:, 0:width], AX.X,
                                      ALU.max).then_inc(max_read, 1)
                    if (j, qt, u) == (HPP - 1, TPB - 1, parts(shape_of(nxt)) - 1):
                        dve.wait_ge(max_read, n + 1)
                        dve.tensor_reduce(mxr[:, p % 2, :, :], mx[:, p % 2, :, :, 0:parts(shape_of(nxt))],
                                          AX.X, ALU.max).then_inc(mx_ready, 1)
                    return neg

                state = [0]

                def body(qb, nxt):
                    if nxt is not None:
                        for k, item in enumerate(items(shape_of(nxt))):
                            state[0] = max_item(nxt, k, item, state[0])
                    if qb is not None:
                        dve.wait_ge(sel_ready, START + qb + 1)
                        dve.reciprocal(rden[:, :], ps[:, S_BANK + 1, :]).then_inc(sel_rden, 1)
                        dve.wait_ge(sel_rden, qb + 1)
                        dve.tensor_tensor(OT[:, q_cols(qb, 0, BLK)], ps[:, S_BANK, :], rden[:, :],
                                          ALU.mult).then_inc(sel_read, 1)
                blocks(dve, body)


def routing(dve, act_pair, chain, lg, prob, cand, pick, comb, rank, small, n_exp, top2):
    E = rank.shape[2]
    e_in, e_out = act_pair
    m, r, v2, g1, g2 = (small[:, i, :] for i in range(5))

    def wide(v):
        return v.unsqueeze(2).broadcast_to([P, NT, E])

    def step(ins):
        chain.link(ins)
        chain.settle()

    def first_of(values, top, out):
        step(dve.tensor_tensor(cand[:, :, :], values, wide(top), ALU.is_equal))
        step(dve.tensor_tensor(cand[:, :, :], cand[:, :, :], rank[:, :, :], ALU.mult))
        step(dve.tensor_reduce(v2, cand[:, :, :], AX.X, ALU.max))
        step(dve.tensor_tensor(out, rank[:, :, :], wide(v2), ALU.is_equal))

    step(dve.tensor_reduce(m, lg, AX.X, ALU.max))
    if not top2:
        first_of(lg, m, comb)
        return
    step(dve.tensor_tensor(prob[:, :, :], lg, wide(m), ALU.subtract))
    dve.sem_inc(e_in, 1)
    dve.wait_ge(e_out, 1)
    step(dve.tensor_reduce(r, prob[:, :, :], AX.X, ALU.add))
    step(dve.reciprocal(r, r))
    step(dve.tensor_tensor(prob[:, :, :], prob[:, :, :], wide(r), ALU.mult))
    step(dve.tensor_reduce(m, prob[:, :, :], AX.X, ALU.max))
    first_of(prob[:, :, :], m, pick[:, 0])
    step(dve.scalar_tensor_tensor(out=prob[:, :, :], in0=pick[:, 0], scalar=-2.0, in1=prob[:, :, :],
                                  op0=ALU.mult, op1=ALU.add))
    step(dve.tensor_reduce(r, prob[:, :, :], AX.X, ALU.max))
    first_of(prob[:, :, :], r, pick[:, 1])
    step(dve.tensor_tensor(g2, r, m, ALU.subtract))
    dve.sem_inc(e_in, 1)
    dve.wait_ge(e_out, 2)
    step(dve.tensor_scalar(g1, g2, 1.0, None, ALU.add))
    step(dve.reciprocal(g1, g1))
    step(dve.tensor_tensor(g2, g2, g1, ALU.mult))
    step(dve.tensor_tensor(pick[:, 0], pick[:, 0], wide(g1), ALU.mult))
    step(dve.tensor_tensor(pick[:, 1], pick[:, 1], wide(g2), ALU.mult))
    step(dve.tensor_tensor(comb, pick[:, 0], pick[:, 1], ALU.add))


def project_norm_route(core, tag, OT, X, hT, comb, dram, E, post_norm, bias, top2):
    nc, ps = core.nc, core.psum
    with ExitStack() as st:
        sem = lambda n: core.sem(st, f"{tag}_{n}")
        sb = lambda n, s, dt=F32: core.sb(st, f"{tag}_{n}", s, dt)
        wo, gamma, beta, rw = sb("wo", [P, P]), sb("gamma", [P, 1]), sb("beta", [P, 1]), sb("rw", [P, E])
        bo = sb("bo", [P, P]) if bias else None
        rank = sb("rank", [P, NT, E])
        N = sb("N", [P, NT, P])
        stats = (sb("stats", [P, NT, 6]), sb("mv", [P, NT, 2]), sb("veps", [P, NT]), sb("rstd", [P, NT]))
        half = sb("half", [P, NT])
        lg, prob, cand = (sb(n, [P, NT, E]) for n in ("lg", "prob", "cand"))
        pick = sb("pick", [P, 2, NT, E])
        small = sb("small", [P, 5, NT])
        w_in, y_ready, n_ready, turned, h_ready, lg_ready = (
            sem(n) for n in ("w_in", "y_ready", "n_ready", "turned", "h_ready", "lg_ready"))
        var_ready, rstd_ready, half_set, e_in, e_out = (
            sem(n) for n in ("var_ready", "rstd_ready", "half_set", "e_in", "e_out"))
        loads = [(wo[:, :], dram["wo"]), (gamma[:, :], dram["gamma"]), (beta[:, :], dram["beta"]),
                 (rw[:, :], dram["rw"]), (rank[:, :, :], dram["rank"])]
        if bias:
            loads.append((bo[:, :], dram["bo"]))
        with nc.Block() as block:
            @block.sync
            def _(sp):
                for dst, src in loads:
                    sp.dma_start(dst, src).then_inc(w_in, 16)

            @block.gpsimd
            def _(pool):
                pool.memset(half[:, :], -0.5).then_inc(half_set, 1)
                pool.wait_ge(half_set, 1)
                for n in range(1 + bool(post_norm)):
                    rsqrt_pool(pool, stats, half, var_ready, rstd_ready, n + 1)

            @block.tensor
            def _(pe):
                pe.wait_ge(w_in, 16 * len(loads))
                for g in range(NB):
                    for i in range(TPB):
                        t = g * TPB + i
                        mm = pe.matmul(ps[:, g, i * P:(i + 1) * P], OT[:, t * P:(t + 1) * P], wo[:, :],
                                       start=True, stop=True)
                    mm.then_inc(y_ready, 1)
                for g in range(NB):
                    pe.wait_ge(n_ready, 1)
                    for i in range(TPB):
                        t = g * TPB + i
                        mm = pe.transpose(ps[:, 4 + g % 2, i * P:(i + 1) * P], N[:, t, :], core.ident[:, :])
                    mm.then_inc(turned, 1)
                    if g >= 1:
                        pe.wait_ge(h_ready, g)
                pe.wait_ge(h_ready, NB)
                for t in range(NT):
                    mm = pe.matmul(ps[:, 6, t * E:(t + 1) * E], hT[:, t * P:(t + 1) * P], rw[:, :],
                                   start=True, stop=True)
                mm.then_inc(lg_ready, 1)

            @block.scalar
            def _(act):
                if top2:
                    act.wait_ge(e_in, 1)
                    act.activation(prob[:, :, :], prob[:, :, :], ACT.Exp).then_inc(e_out, 1)
                    act.wait_ge(e_in, 2)
                    act.activation(small[:, 4, :], small[:, 4, :], ACT.Exp).then_inc(e_out, 1)

            @block.vector
            def _(dve):
                chain = Chain(dve, sem("chain"))
                dve.wait_ge(w_in, 16 * len(loads))
                for t in range(NT):
                    if bias:
                        chain.link(dve.tensor_tensor(X[:, t, :], X[:, t, :], bo[:, :], ALU.add))
                chain.settle()
                for g in range(NB):
                    dve.wait_ge(y_ready, g + 1)
                    mine = X[:, g * TPB:(g + 1) * TPB, :]
                    chain.link(dve.tensor_tensor(mine, ps[:, g, :].rearrange("p (t c) -> p t c", c=P), mine, ALU.add))
                chain.settle()
                n = 0
                if post_norm:
                    n += 1
                    layer_norm(dve, chain, X, X, stats, (var_ready,), (rstd_ready, n), range(NT))
                n += 1
                layer_norm(dve, chain, X, N, stats, (var_ready,), (rstd_ready, n), range(NT))
                dve.sem_inc(n_ready, 1)
                for g in range(NB):
                    dve.wait_ge(turned, g + 1)
                    dve.tensor_scalar(hT[:, g * BLK:(g + 1) * BLK], ps[:, 4 + g % 2, :], gamma[:, 0:1], beta[:, 0:1],
                                      ALU.mult, ALU.add).then_inc(h_ready, 1)
                dve.wait_ge(lg_ready, 1)
                chain.link(dve.tensor_copy(lg[:, :, :], ps[:, 6, 0:NT * E].rearrange("p (t e) -> p t e", e=E)))
                chain.settle()
                routing(dve, (e_in, e_out), chain, lg[:, :, :], prob, cand, pick, comb[:, :, 0:E], rank, small, 0, top2)
                if top2:
                    chain.link(dve.memset(comb[:, :, E:E + 1], 1.0))
                chain.settle()


def experts(core, tag, hT, comb, acc, gate_up, down, E, NF, shared):
    nc, ps = core.nc, core.psum
    F = NF * P
    with ExitStack() as st:
        sem = lambda n: core.sem(st, f"{tag}_{n}")
        sb = lambda n, s, dt=F32: core.sb(st, f"{tag}_{n}", s, dt)
        wgu = sb("wgu", [P, 2, 2 * F])
        wd = sb("wd", [P, 2, NF, P])
        sgu, sd = (sb("sgu", [P, 2 * P]), sb("sd", [P, P])) if shared else (None, None)
        gate = sb("gate", [P, 2, BLK])
        prod = sb("prod", [P, 2, NF, BLK])
        w_in = [sem("w_in0"), sem("w_in1")]
        s_in = sem("s_in")
        gu_ready, gu_free, silu_done, prod_ready = (sem(n) for n in ("gu_ready", "gu_free", "silu_done", "prod_ready"))
        y_ready, y_free = sem("y_ready"), sem("y_free")
        UNITS = 2 * NB
        PAIRS = E // 2

        with nc.Block() as block:
            @block.sync
            def _(sp):
                def load(slot, e):
                    one = slice(e, e + 1) if isinstance(e, int) else bass.ds(e, 1)
                    sp.dma_start(wgu[:, slot, :], gate_up[one].rearrange("o d f -> (o d) f")).then_inc(w_in[slot], 16)
                    sp.dma_start(wd[:, slot, :, :], down[one].rearrange("o (c p) n -> p (o c) n", p=P)).then_inc(w_in[slot], 16)
                load(0, 0)
                load(1, 1)
                if shared:
                    sp.dma_start(sgu[:, :], shared[0]).then_inc(s_in, 16)
                    sp.dma_start(sd[:, :], shared[1]).then_inc(s_in, 16)
                with sp.Fori(0, PAIRS - 1) as it:
                    for slot in range(2):
                        sp.wait_ge(y_ready, it * UNITS + NB * (slot + 1))
                        load(slot, it * 2 + 2 + slot)

            @block.tensor
            def _(pe):
                def up(wts, nf, n, u, b):
                    for c in range(nf):
                        pe.wait_ge(gu_free, n + c + 1)
                        bank = 2 * ((u * nf + c) % 2)
                        cols = hT[:, b * BLK:(b + 1) * BLK]
                        pe.matmul(ps[:, bank, :], wts[:, c * P:(c + 1) * P], cols, start=True, stop=True)
                        pe.matmul(ps[:, bank + 1, :], wts[:, (nf + c) * P:(nf + c + 1) * P], cols,
                                  start=True, stop=True).then_inc(gu_ready, 1)

                def dn(wts, nf, n, u, m):
                    pe.wait_ge(prod_ready, n + nf)
                    pe.wait_ge(y_free, m + 1)
                    for i in range(TPB):
                        for c in range(nf):
                            mm = pe.matmul(ps[:, 4 + u % 2, i * P:(i + 1) * P], prod[:, u % 2, c, i * P:(i + 1) * P],
                                           wts(c), start=(c == 0), stop=(c == nf - 1))
                    mm.then_inc(y_ready, 1)

                with pe.Fori(0, PAIRS) as it:
                    n0, m0 = it * (UNITS * NF), it * UNITS
                    for u in range(UNITS):
                        slot = u // NB
                        if u % NB == 0:
                            pe.wait_ge(w_in[slot], it * 32 + 32)
                        up(wgu[:, slot, :], NF, n0 + u * NF, u, u % NB)
                        if u >= 1:
                            v = u - 1
                            dn(lambda c: wd[:, v // NB, c, :], NF, n0 + v * NF, v, m0 + v)
                    v = UNITS - 1
                    dn(lambda c: wd[:, v // NB, c, :], NF, n0 + v * NF, v, m0 + v)
                if shared:
                    n0, m0 = PAIRS * UNITS * NF, PAIRS * UNITS
                    pe.wait_ge(s_in, 32)
                    for u in range(NB):
                        up(sgu[:, :], 1, n0 + u, u, u)
                        if u >= 1:
                            dn(lambda c: sd[:, :], 1, n0 + u - 1, u - 1, m0 + u - 1)
                    dn(lambda c: sd[:, :], 1, n0 + NB - 1, NB - 1, m0 + NB - 1)

            @block.scalar
            def _(act):
                def silu(nf, n, u):
                    for c in range(nf):
                        k = (u * nf + c) % 2
                        act.wait_ge(gu_ready, n + c + 1)
                        act.wait_ge(gu_free, n + c + 1)
                        act.activation(gate[:, k, :], ps[:, 2 * k, :], ACT.Silu).then_inc(silu_done, 1)
                with act.Fori(0, PAIRS) as it:
                    for u in range(UNITS):
                        silu(NF, it * (UNITS * NF) + u * NF, u)
                if shared:
                    for u in range(NB):
                        silu(1, PAIRS * UNITS * NF + u, u)

            @block.vector
            def _(dve):
                dve.memset(acc[:, 0:NT // 2, :], 0.0).then_inc(gu_free, 2)
                dve.memset(acc[:, NT // 2:, :], 0.0).then_inc(y_free, 2)

                def mult(nf, n, u):
                    for c in range(nf):
                        k = (u * nf + c) % 2
                        dve.wait_ge(silu_done, n + c + 1)
                        dve.tensor_tensor(prod[:, u % 2, c, :], gate[:, k, :], ps[:, 2 * k + 1, :],
                                          ALU.mult).then_inc(prod_ready, 1)
                        dve.wait_ge(prod_ready, n + c + 1)
                        dve.sem_inc(gu_free, 1)

                def gather(m, u, b, e):
                    dve.wait_ge(y_ready, m + 1)
                    one = slice(e, e + 1) if isinstance(e, int) else bass.ds(e, 1)
                    for i in range(TPB):
                        t = b * TPB + i
                        ins = dve.scalar_tensor_tensor(out=acc[:, t, :], in0=ps[:, 4 + u % 2, i * P:(i + 1) * P],
                                                       scalar=comb[:, t, one], in1=acc[:, t, :],
                                                       op0=ALU.mult, op1=ALU.add)
                    ins.then_inc(y_free, 1)
                dve.wait_ge(gu_free, 2)
                dve.wait_ge(y_free, 2)
                with dve.Fori(0, PAIRS) as it:
                    for u in range(UNITS):
                        mult(NF, it * (UNITS * NF) + u * NF, u)
                        if u >= 1:
                            gather(it * UNITS + u - 1, u - 1, (u - 1) % NB, it * 2 + (u - 1) // NB)
                    u = UNITS - 1
                    gather(it * UNITS + u, u, u % NB, it * 2 + u // NB)
                if shared:
                    for u in range(NB):
                        mult(1, PAIRS * UNITS * NF + u, u)
                        if u >= 1:
                            gather(PAIRS * UNITS + u - 1, u - 1, u - 1, E)
                    gather(PAIRS * UNITS + NB - 1, NB - 1, NB - 1, E)


def norm_l2_norm(core, tag, X, acc, xnT, dram):
    nc, ps = core.nc, core.psum
    with ExitStack() as st:
        sem = lambda n: core.sem(st, f"{tag}_{n}")
        sb = lambda n, s, dt=F32: core.sb(st, f"{tag}_{n}", s, dt)
        gamma = sb("gamma", [P, 1])
        stats = (sb("stats", [P, NT, 6]), sb("mv", [P, NT, 2]), sb("veps", [P, NT]), sb("rstd", [P, NT]))
        half = sb("half", [P, 2, NT])
        N = sb("N", [P, NT, P])
        sq, inv = sb("sq", [P, NT]), sb("inv", [P, NT])
        g_in, var_ready, rstd_ready, half_set = (sem(n) for n in ("g_in", "var_ready", "rstd_ready", "half_set"))
        sq_ready, root_ready, n_ready, turned, h_ready = (
            sem(n) for n in ("sq_ready", "root_ready", "n_ready", "turned", "h_ready"))
        with nc.Block() as block:
            @block.sync
            def _(sp):
                sp.dma_start(gamma[:, :], dram["gamma"]).then_inc(g_in, 16)

            @block.gpsimd
            def _(pool):
                pool.memset(half[:, 0, :], -0.5).then_inc(half_set, 1)
                pool.wait_ge(half_set, 1)
                pool.memset(half[:, 1, :], 0.5).then_inc(half_set, 1)
                pool.wait_ge(half_set, 2)
                rsqrt_pool(pool, stats, half[:, 0, :], var_ready, rstd_ready, 1)
                pool.wait_ge(sq_ready, 1)
                pool.tensor_tensor(inv[:, :], sq[:, :], half[:, 1, :], ALU.pow).then_inc(root_ready, 1)

            @block.tensor
            def _(pe):
                pe.wait_ge(n_ready, 1)
                for g in range(NB):
                    for i in range(TPB):
                        mm = pe.transpose(ps[:, g, i * P:(i + 1) * P], N[:, g * TPB + i, :], core.ident[:, :])
                    mm.then_inc(turned, 1)

            @block.vector
            def _(dve):
                chain = Chain(dve, sem("chain"))
                for g in range(NB):
                    mine = slice(g * TPB, (g + 1) * TPB)
                    chain.link(dve.tensor_tensor(X[:, mine, :], X[:, mine, :], acc[:, mine, :], ALU.add))
                chain.settle()
                layer_norm(dve, chain, X, X, stats, (var_ready,), (rstd_ready, 1), range(NT))
                chain.link(dve.tensor_tensor(N[:, :, :], X[:, :, :], X[:, :, :], ALU.mult))
                chain.settle()
                dve.tensor_reduce(sq[:, :], N[:, :, :], AX.X, ALU.add).then_inc(sq_ready, 1)
                dve.wait_ge(root_ready, 1)
                chain.link(dve.tensor_scalar(inv[:, :], inv[:, :], 1e-12, None, ALU.max))
                chain.settle()
                chain.link(dve.reciprocal(inv[:, :], inv[:, :]))
                chain.settle()
                for t in range(NT):
                    chain.link(dve.tensor_scalar(N[:, t, :], X[:, t, :], inv[:, t:t + 1], float(P) ** 0.5,
                                                 ALU.mult, ALU.mult))
                chain.settle()
                dve.sem_inc(n_ready, 1)
                dve.wait_ge(g_in, 16)
                for g in range(NB):
                    dve.wait_ge(turned, g + 1)
                    dve.tensor_scalar(xnT[:, g * BLK:(g + 1) * BLK], ps[:, g, :], gamma[:, 0:1], None,
                                      ALU.mult).then_inc(h_ready, 1)


def big_head_values(core, tag, xnT, V, wv_dram):
    nc, ps = core.nc, core.psum
    W = BIG_HEADS * BIG_HD
    with ExitStack() as st:
        wv = core.sb(st, f"{tag}_wv", [P, W])
        w_in, v_ready, va_read, vd_read = (core.sem(st, f"{tag}_{n}") for n in ("w_in", "v_ready", "va_read", "vd_read"))
        jobs = [(t, c) for t in range(NT) for c in range(W // BLK)]
        with nc.Block() as block:
            @block.sync
            def _(sp):
                sp.dma_start(wv[:, :], wv_dram).then_inc(w_in, 16)

            @block.tensor
            def _(pe):
                pe.wait_ge(w_in, 16)
                for n, (t, c) in enumerate(jobs):
                    if n >= 4:
                        pe.wait_ge(vd_read if n % 2 == 0 else va_read, n // 2 - 1)
                    pe.matmul(ps[:, n % 4, :], xnT[:, t * P:(t + 1) * P], wv[:, c * BLK:(c + 1) * BLK],
                              start=True, stop=True).then_inc(v_ready, 1)

            @block.vector
            def _(dve):
                for n, (t, c) in list(enumerate(jobs))[0::2]:
                    dve.wait_ge(v_ready, n + 1)
                    dve.tensor_copy(V[:, t, c * BLK:(c + 1) * BLK], ps[:, n % 4, :]).then_inc(vd_read, 1)

            @block.scalar
            def _(act):
                for n, (t, c) in list(enumerate(jobs))[1::2]:
                    act.wait_ge(v_ready, n + 1)
                    act.activation(V[:, t, c * BLK:(c + 1) * BLK], ps[:, n % 4, :], ACT.Copy).then_inc(va_read, 1)


def big_head_attention(core, tag, xnT, V, O, wqk_dram, diag_neg):
    nc, ps = core.nc, core.psum
    scale = float(BIG_HD) ** -0.5
    chunks = [(i + TPB) // TPB for i in range(NT)]
    upto = [sum(chunks[:i]) for i in range(NT + 1)]
    NC = upto[-1]
    NPJ = 2 * NB
    PT_SLOTS = 4

    def bank0(i):
        return 2 * (i % 2) if chunks[i] <= 2 else 0

    with ExitStack() as st:
        sem = lambda n: core.sem(st, f"{tag}_{n}")
        sb = lambda n, s, dt=F32: core.sb(st, f"{tag}_{n}", s, dt)
        W = sb("W", [P, BIG_HEADS * 2 * BIG_HD])
        wcur = sb("wcur", [P, 2 * BIG_HD])
        KQ = sb("KQ", [P, 2, T])
        probs = sb("probs", [P, 2, T])
        PT = sb("PT", [P, PT_SLOTS, BLK])
        mxc, m = sb("mxc", [P, 4]), sb("m", [P, 1])
        negm, total, rec = sb("negm", [P, 2]), sb("total", [P, 2]), sb("rec", [P, 2])
        w_in, w_cur, pj_ready, k_done, q_done = (sem(n) for n in ("w_in", "w_cur", "pj_ready", "k_done", "q_done"))
        s_ready, neg_done, mx_step, negm_ready, exp_done = (
            sem(n) for n in ("s_ready", "neg_done", "mx_step", "negm_ready", "exp_done"))
        turned, pt_done, av_done, rec_ready, o_done = (
            sem(n) for n in ("turned", "pt_done", "av_done", "rec_ready", "o_done"))
        mx_per_head = NC + sum(c > 1 for c in chunks)

        with nc.Block() as block:
            @block.sync
            def _(sp):
                sp.dma_start(W[:, :], wqk_dram).then_inc(w_in, 16)

            @block.tensor
            def _(pe):
                start_counts(pe, pj_ready, turned, av_done)
                with pe.Fori(0, BIG_HEADS) as h:
                    pe.wait_ge(w_cur, h + 1)
                    pe.wait_ge(pt_done, START + h * NC)
                    pe.wait_ge(o_done, START + h * NT)
                    for n in range(NPJ):
                        if n >= 4:
                            pe.wait_ge(k_done if n % 2 == 0 else q_done, h * NB + (n // 2 - 1))
                        pe.matmul(ps[:, 4 + n % 4, :], wcur[:, (1 - n % 2) * P:(2 - n % 2) * P],
                                  xnT[:, (n // 2) * BLK:(n // 2 + 1) * BLK], start=True, stop=True).then_inc(pj_ready, 1)

                    def scores(i):
                        if chunks[i] <= 2:
                            pe.wait_ge(exp_done, START + h * NT + max(i - 1, 0))
                        else:
                            pe.wait_ge(exp_done, START + h * NT + i)
                        if i == 0 or chunks[i] != chunks[i - 1]:
                            pe.wait_ge(k_done, h * NB + chunks[i])
                            pe.wait_ge(q_done, h * NB + chunks[i])
                        for c in range(chunks[i]):
                            w = min(BLK, (i + 1) * P - c * BLK)
                            pe.matmul(ps[:, bank0(i) + c, 0:w], KQ[:, 1, i * P:(i + 1) * P],
                                      KQ[:, 0, c * BLK:c * BLK + w], start=True, stop=True).then_inc(s_ready, 1)

                    def turn(i, c):
                        k = upto[i] + c
                        if c == 0:
                            pe.wait_ge(exp_done, START + h * NT + i + 1)
                        if k >= 2:
                            pe.wait_ge(pt_done, START + h * NC + (k - 1))
                        else:
                            pe.wait_ge(k_done, h * NB + NB)
                            pe.wait_ge(q_done, h * NB + NB)
                        for j in range(min(TPB, i + 1 - TPB * c)):
                            kt = TPB * c + j
                            mm = pe.transpose(ps[:, 4 + k % 2, j * P:(j + 1) * P],
                                              probs[:, i % 2, kt * P:(kt + 1) * P], core.ident[:, :])
                        mm.then_inc(turned, 1)

                    def product(i, c):
                        k = upto[i] + c
                        pe.wait_ge(pt_done, START + h * NC + (k + 1))
                        if c == 0 and i >= 2:
                            pe.wait_ge(o_done, START + h * NT + (i - 1))
                        for j in range(min(TPB, i + 1 - TPB * c)):
                            kt = TPB * c + j
                            mm = pe.matmul(ps[:, 6 + i % 2, 0:P], PT[:, k % PT_SLOTS, j * P:(j + 1) * P],
                                           V[:, kt, bass.ds(h * P, P)], start=(kt == 0), stop=(kt == i))
                        mm.then_inc(av_done, 1)

                    def finish(i):
                        turn(i, 0)
                        for c in range(chunks[i]):
                            if c + 1 < chunks[i]:
                                turn(i, c + 1)
                            product(i, c)

                    scores(0)
                    for i in range(1, NT):
                        scores(i)
                        finish(i - 1)
                    finish(NT - 1)

            @block.vector
            def _(dve):
                start_counts(dve, pt_done)
                dve.wait_ge(w_in, 16)
                with dve.Fori(0, BIG_HEADS) as h:
                    dve.wait_ge(pj_ready, START + h * NPJ)
                    dve.tensor_copy(wcur[:, :], W[:, bass.ds(h * (2 * P), 2 * P)]).then_inc(w_cur, 1)
                    for n in range(0, NPJ, 2):
                        dve.wait_ge(pj_ready, START + h * NPJ + (n + 1))
                        dve.tensor_copy(KQ[:, 0, (n // 2) * BLK:(n // 2 + 1) * BLK], ps[:, 4 + n % 4, :]).then_inc(k_done, 1)
                    done = 0

                    def evac(i):
                        for c in range(chunks[i]):
                            k = upto[i] + c
                            w = min(BLK, (i + 1) * P - c * BLK)
                            dve.wait_ge(turned, START + h * NC + (k + 1))
                            dve.wait_ge(av_done, START + h * NC + max(k - PT_SLOTS + 1, 0))
                            dve.tensor_copy(PT[:, k % PT_SLOTS, 0:w], ps[:, 4 + k % 2, 0:w]).then_inc(pt_done, 1)
                        dve.wait_ge(o_done, START + h * NT + max(i - 1, 0))
                        dve.wait_ge(exp_done, START + h * NT + (i + 1))
                        dve.reciprocal(rec[:, i % 2:i % 2 + 1], total[:, i % 2:i % 2 + 1]).then_inc(rec_ready, 1)

                    for i in range(NT):
                        for c in range(chunks[i]):
                            w = min(BLK, (i + 1) * P - c * BLK)
                            dve.wait_ge(s_ready, h * NC + (upto[i] + c + 1))
                            bank = ps[:, bank0(i) + c, :]
                            if c == chunks[i] - 1:
                                diag = bank[:, w - P:w]
                                dve.tensor_tensor(diag, diag, diag_neg[:, :], ALU.add).then_inc(neg_done, 1)
                                dve.wait_ge(neg_done, h * NT + (i + 1))
                            dve.tensor_reduce(mxc[:, c:c + 1], bank[:, 0:w], AX.X, ALU.max).then_inc(mx_step, 1)
                            done += 1
                        top = mxc[:, 0:1]
                        dve.wait_ge(mx_step, h * mx_per_head + done)
                        if chunks[i] > 1:
                            dve.tensor_reduce(m[:, :], mxc[:, 0:chunks[i]], AX.X, ALU.max).then_inc(mx_step, 1)
                            done += 1
                            dve.wait_ge(mx_step, h * mx_per_head + done)
                            top = m[:, :]
                        dve.tensor_scalar(negm[:, i % 2:i % 2 + 1], top, -scale, None, ALU.mult).then_inc(negm_ready, 1)
                        if i >= 1:
                            evac(i - 1)
                    evac(NT - 1)

            @block.scalar
            def _(act):
                start_counts(act, exp_done, o_done)
                with act.Fori(0, BIG_HEADS) as h:
                    for n in range(1, NPJ, 2):
                        act.wait_ge(pj_ready, START + h * NPJ + (n + 1))
                        act.activation(KQ[:, 1, (n // 2) * BLK:(n // 2 + 1) * BLK], ps[:, 4 + n % 4, :],
                                       ACT.Copy).then_inc(q_done, 1)

                    def out(i):
                        act.wait_ge(av_done, START + h * NC + upto[i + 1])
                        act.wait_ge(rec_ready, h * NT + (i + 1))
                        act.activation(O[:, i, bass.ds(h * P, P)], ps[:, 6 + i % 2, 0:P], ACT.Copy,
                                       scale=rec[:, i % 2:i % 2 + 1]).then_inc(o_done, 1)

                    for i in range(NT):
                        w = (i + 1) * P
                        act.wait_ge(negm_ready, h * NT + (i + 1))
                        act.wait_ge(turned, START + h * NC + upto[max(i - 1, 0)])
                        banks = ps[:, bank0(i):bank0(i) + chunks[i], :].rearrange("p b n -> p (b n)")
                        act.activation(probs[:, i % 2, 0:w], banks[:, 0:w], ACT.Exp, bias=negm[:, i % 2:i % 2 + 1],
                                       scale=scale, accum_out=total[:, i % 2:i % 2 + 1]).then_inc(exp_done, 1)
                        if i >= 1:
                            out(i - 1)
                    out(NT - 1)


def big_head_output_conv(core, tag, O, X, cT, dram):
    nc, ps = core.nc, core.psum
    with ExitStack() as st:
        sem = lambda n: core.sem(st, f"{tag}_{n}")
        sb = lambda n, s, dt=F32: core.sb(st, f"{tag}_{n}", s, dt)
        wo = sb("wo", [P, BIG_HEADS, P])
        gamma, beta, cw = sb("gamma", [P, 1]), sb("beta", [P, 1]), sb("cw", [P, 3])
        OTt = sb("OTt", [P, 2, BIG_HEADS, P])
        N = sb("N", [P, NT, P])
        hpad = sb("hpad", [P, T + 2])
        stats = (sb("stats", [P, NT, 6]), sb("mv", [P, NT, 2]), sb("veps", [P, NT]), sb("rstd", [P, NT]))
        half = sb("half", [P, NT])
        w_in, pad_set, turned, ot_a, ot_d, y_ready, y_read = (
            sem(n) for n in ("w_in", "pad_set", "turned", "ot_a", "ot_d", "y_ready", "y_read"))
        var_ready, rstd_ready, half_set, n_ready, n_turned, h_ready = (
            sem(n) for n in ("var_ready", "rstd_ready", "half_set", "n_ready", "n_turned", "h_ready"))
        loads = [(wo[:, :, :], dram["wo"]), (gamma[:, :], dram["gamma"]), (beta[:, :], dram["beta"]), (cw[:, :], dram["cw"])]
        with nc.Block() as block:
            @block.sync
            def _(sp):
                for dst, src in loads:
                    sp.dma_start(dst, src).then_inc(w_in, 16)

            @block.gpsimd
            def _(pool):
                pool.memset(hpad[:, 0:2], 0.0).then_inc(pad_set, 1)
                pool.wait_ge(pad_set, 1)
                pool.memset(half[:, :], -0.5).then_inc(half_set, 1)
                pool.wait_ge(half_set, 1)
                for n in range(2):
                    rsqrt_pool(pool, stats, half, var_ready, rstd_ready, n + 1)

            @block.tensor
            def _(pe):
                pe.wait_ge(w_in, 16 * len(loads))

                def turn(t):
                    if t >= 2:
                        pe.wait_ge(ot_d, t - 1)
                        pe.wait_ge(ot_a, t - 1)
                    for f in range(BIG_HEADS):
                        mm = pe.transpose(ps[:, 2 * (t % 2) + f // 4, (f % 4) * P:(f % 4 + 1) * P],
                                          O[:, t, f * P:(f + 1) * P], core.ident[:, :])
                    mm.then_inc(turned, 1)

                def out(t):
                    pe.wait_ge(ot_d, t + 1)
                    pe.wait_ge(ot_a, t + 1)
                    if t >= 2:
                        pe.wait_ge(y_read, t - 1)
                    for f in range(BIG_HEADS):
                        mm = pe.matmul(ps[:, 4 + t % 2, 0:P], OTt[:, t % 2, f, :], wo[:, f, :],
                                       start=(f == 0), stop=(f == BIG_HEADS - 1))
                    mm.then_inc(y_ready, 1)

                turn(0)
                for t in range(1, NT):
                    turn(t)
                    out(t - 1)
                out(NT - 1)
                pe.wait_ge(n_ready, 1)
                for g in range(NB):
                    for i in range(TPB):
                        mm = pe.transpose(ps[:, g, i * P:(i + 1) * P], N[:, g * TPB + i, :], core.ident[:, :])
                    mm.then_inc(n_turned, 1)

            @block.scalar
            def _(act):
                for t in range(NT):
                    act.wait_ge(turned, t + 1)
                    if t >= 2:
                        act.wait_ge(y_ready, t - 1)
                    act.activation(OTt[:, t % 2, 4:8, :].rearrange("p f n -> p (f n)"), ps[:, 2 * (t % 2) + 1, :],
                                   ACT.Copy).then_inc(ot_a, 1)

            @block.vector
            def _(dve):
                chain = Chain(dve, sem("chain"))

                def add(t):
                    dve.wait_ge(y_ready, t + 1)
                    dve.tensor_tensor(X[:, t, :], ps[:, 4 + t % 2, 0:P], X[:, t, :], ALU.add).then_inc(y_read, 1)
                for t in range(NT):
                    dve.wait_ge(turned, t + 1)
                    if t >= 2:
                        dve.wait_ge(y_ready, t - 1)
                    dve.tensor_copy(OTt[:, t % 2, 0:4, :].rearrange("p f n -> p (f n)"),
                                    ps[:, 2 * (t % 2), :]).then_inc(ot_d, 1)
                    if t >= 1:
                        add(t - 1)
                add(NT - 1)
                dve.wait_ge(y_read, NT)
                layer_norm(dve, chain, X, X, stats, (var_ready,), (rstd_ready, 1), range(NT))
                layer_norm(dve, chain, X, N, stats, (var_ready,), (rstd_ready, 2), range(NT))
                dve.sem_inc(n_ready, 1)
                dve.wait_ge(w_in, 16 * len(loads))
                for g in range(NB):
                    dve.wait_ge(n_turned, g + 1)
                    chain.link(dve.tensor_scalar(hpad[:, 2 + g * BLK:2 + (g + 1) * BLK], ps[:, g, :], gamma[:, 0:1],
                                                 beta[:, 0:1], ALU.mult, ALU.add))
                chain.settle()
                dve.wait_ge(pad_set, 1)
                chain.link(dve.tensor_scalar(cT[:, :], hpad[:, 0:T], cw[:, 0:1], None, ALU.mult))
                chain.settle()
                for k in (1, 2):
                    chain.link(dve.scalar_tensor_tensor(out=cT[:, :], in0=hpad[:, k:k + T], scalar=cw[:, k:k + 1],
                                                        in1=cT[:, :], op0=ALU.mult, op1=ALU.add))
                    chain.settle()


def final_norm(core, tag, X, XA, acc, out):
    nc = core.nc
    with ExitStack() as st:
        sem = lambda n: core.sem(st, f"{tag}_{n}")
        sb = lambda n, s, dt=F32: core.sb(st, f"{tag}_{n}", s, dt)
        stats = (sb("stats", [P, NT, 6]), sb("mv", [P, NT, 2]), sb("veps", [P, NT]), sb("rstd", [P, NT]))
        half = sb("half", [P, NT])
        var_ready, rstd_ready, half_set, done, stored = (
            sem(n) for n in ("var_ready", "rstd_ready", "half_set", "done", "stored"))
        with nc.Block() as block:
            @block.gpsimd
            def _(pool):
                pool.memset(half[:, :], -0.5).then_inc(half_set, 1)
                pool.wait_ge(half_set, 1)
                rsqrt_pool(pool, stats, half, var_ready, rstd_ready, 1)

            @block.vector
            def _(dve):
                chain = Chain(dve, sem("chain"))
                for other in (XA, X):
                    for g in range(NB):
                        mine = slice(g * TPB, (g + 1) * TPB)
                        chain.link(dve.tensor_tensor(acc[:, mine, :], acc[:, mine, :], other[:, mine, :], ALU.add))
                    chain.settle()
                layer_norm(dve, chain, acc, acc, stats, (var_ready,), (rstd_ready, 1), range(NT))
                dve.sem_inc(done, 1)

            @block.sync
            def _(sp):
                sp.wait_ge(done, 1)
                sp.dma_start(out.rearrange("(t p) c -> p t c", p=P), acc[:, :, :]).then_inc(stored, 16)
                sp.wait_ge(stored, 16)


def load_start(core, pairs):
    with ExitStack() as st:
        loaded = core.sem(st, "start_loaded")
        with core.nc.Block() as block:
            @block.sync
            def _(sp):
                for dst, src in pairs:
                    sp.dma_start(dst, src).then_inc(loaded, 16)
                sp.wait_ge(loaded, 16 * len(pairs))


def copy_tokens(core, tag, src, dst):
    with ExitStack() as st:
        copied = core.sem(st, f"{tag}_copied")
        with core.nc.Block() as block:
            @block.vector
            def _(dve):
                dve.tensor_copy(dst[:, :, :], src[:, :, :]).then_inc(copied, 1)


def small_attention(core, tag, src_T, OT, dram, table, causal, biased, scratch, diag_neg):
    with ExitStack() as st:
        KS = core.sb(st, f"{tag}_KS", [ROWS, HEADS, T], BF16)
        QS = core.sb(st, f"{tag}_QS", [ROWS, HEADS, T], BF16)
        V = core.sb(st, f"{tag}_V", [P, NT, HEADS, 2 * HD])
        small_head_projections(core, tag + "p", src_T, dram, KS, QS, V, biased, table, scratch)
        with ExitStack() as st2:
            sel = core.sb(st2, f"{tag}_sel", [P, 2, NPACK, P])
            load_start_sel = [(sel[:, :, :, :], dram["sel"])]
            loaded = core.sem(st2, f"{tag}_sel_in")
            with core.nc.Block() as block:
                @block.sync
                def _(sp):
                    for dst, src in load_start_sel:
                        sp.dma_start(dst, src).then_inc(loaded, 16)
                    sp.wait_ge(loaded, 16)
            small_head_attention(core, tag + "a", KS, QS, V, OT, sel, diag_neg, causal)


def two_layers(nc, a, out):
    scratch = nc.dram_tensor("split_scratch", [2, TERMS, P, BLK], BF16, kind="Internal").ap()
    with ExitStack() as stack:
        core = Core(nc, stack)
        sb = lambda n, s, dt=F32: core.sb(stack, n, s, dt)
        core.ident = sb("ident", [P, P])
        X = sb("X", [P, NT, P])
        AT = sb("AT", [P, T])
        diag_neg = sb("diag_neg", [P, P])
        load_start(core, [(X[:, :, :], a["x"].rearrange("(t p) c -> p t c", p=P)), (AT[:, :], a["xT"]),
                          (core.ident[:, :], a["ident"]), (diag_neg[:, :], a["diag_neg"])])

        small_attention(core, "a0", AT, AT, {**{n: a["l0_" + n] for n in ("wq", "wqr", "wk", "wkr", "wv", "bq",
                        "bqr", "bk", "bkr", "bv")}, "sel": a["sel"]}, a["rope0"], False, True, scratch, diag_neg)
        core.recycle_semaphores()
        with ExitStack() as st:
            comb = core.sb(st, "comb0", [P, NT, 9])
            hT = core.sb(st, "h0T", [P, T])
            acc = core.sb(st, "acc0", [P, NT, P])
            project_norm_route(core, "r0", AT, X, hT, comb, {"wo": a["l0_wo"], "bo": a["l0_bo"], "gamma": a["l0_gamma"],
                               "beta": a["l0_beta"], "rw": a["l0_rw"], "rank": a["rank8"]}, 8, True, True, True)
            experts(core, "e0", hT, comb, acc, a["l0_gate_up"], a["l0_down"], 8, 3, (a["l0_sgu"], a["l0_sd"]))
            norm_l2_norm(core, "n0", X, acc, AT, {"gamma": a["l1_gamma"]})

        core.recycle_semaphores()
        with ExitStack() as st:
            O = core.sb(st, "O1", [P, NT, BIG_HEADS * BIG_HD])
            with ExitStack() as st2:
                V = core.sb(st2, "V1", [P, NT, BIG_HEADS * BIG_HD])
                big_head_values(core, "v1", AT, V, a["l1_big_wv"])
                big_head_attention(core, "b1", AT, V, O, a["l1_wqk"], diag_neg)
            big_head_output_conv(core, "o1", O, X, AT, {"wo": a["l1_wout"].rearrange("(f p) n -> p f n", p=P),
                                 "gamma": a["l1_ln1_w"], "beta": a["l1_ln1_b"], "cw": a["l1_conv"]})

        core.recycle_semaphores()
        small_attention(core, "a1", AT, AT, {**{n: a["l1_" + n] for n in ("wq", "wqr", "wk", "wkr", "wv")},
                        "sel": a["sel"]}, a["rope1"], True, False, scratch, diag_neg)
        with ExitStack() as st:
            XA = core.sb(st, "XA", [P, NT, P])
            comb = core.sb(st, "comb1", [P, NT, 4])
            hT = core.sb(st, "h1T", [P, T])
            acc = core.sb(st, "acc1", [P, NT, P])
            copy_tokens(core, "c1", X, XA)
            project_norm_route(core, "r1", AT, XA, hT, comb, {"wo": a["l1_proj"], "gamma": a["l1_ln2_w"],
                               "beta": a["l1_ln2_b"], "rw": a["l1_rw"], "rank": a["rank4"]}, 4, False, False, False)
            experts(core, "e1", hT, comb, acc, a["l1_gate_up"], a["l1_down"], 4, 4, None)
            final_norm(core, "f1", X, XA, acc, out)


def constants():
    import numpy as np
    f = np.float32
    c = {"ident": np.eye(P, dtype=f)}
    q, k = np.arange(P)[:, None], np.arange(P)[None, :]
    c["diag_neg"] = np.where(k > q, f(NEG), f(0)).astype(f)
    inv = (f(1.0) / np.power(f(10000.0), np.arange(0, HD, 2, dtype=f) / f(HD))).astype(f)
    ang = (np.arange(T, dtype=f)[:, None] * inv[None, :]).astype(f)
    sign = np.where(np.arange(HD) < HD // 2, f(-1), f(1))
    for name, col in (("rope0", np.arange(HD) // 2), ("rope1", np.arange(HD) % (HD // 2))):
        cos = np.cos(ang).astype(f)[:, col].T
        sin = (np.sin(ang).astype(f)[:, col] * sign[None, :]).T
        c[name] = np.ascontiguousarray(np.stack([np.tile(cos, (HEADS, 1)), np.tile(sin, (HEADS, 1))], 1), dtype=f)
    sel = np.zeros((P, 2, NPACK, P), f)
    for p in range(NPACK):
        for j in range(HPP):
            for d in range(HD):
                sel[32 * j + d, 0, p, (HPP * p + j) * HD + d] = 1
                sel[32 * j + HD + d, 1, p, (HPP * p + j) * HD + d] = 1
    c["sel"] = sel
    for e in (8, 4):
        c[f"rank{e}"] = np.broadcast_to(np.arange(e, 0, -1, dtype=f), (P, NT, e)).copy()
    return c


def layouts(i):
    import numpy as np
    t = lambda x: np.ascontiguousarray(np.asarray(x).T)
    col = lambda x: np.ascontiguousarray(np.asarray(x).reshape(P, 1))
    rows = lambda x: np.ascontiguousarray(np.broadcast_to(np.asarray(x).reshape(1, P), (P, P)))
    turn = np.arange(P) // HD * HD + (np.arange(P) % HD + HD // 2) % HD
    x = np.asarray(i["L0_attn_x"]).reshape(T, P)
    d = {"x": np.ascontiguousarray(x), "xT": t(x)}
    for n in "qkv":
        d[f"l0_w{n}"] = t(i[f"L0_attn_w{n}"])
    for n in "qk":
        d[f"l0_w{n}r"] = t(np.asarray(i[f"L0_attn_w{n}"])[turn])
        d[f"l0_b{n}"] = col(i[f"L0_attn_b{n}"])
        d[f"l0_b{n}r"] = col(np.asarray(i[f"L0_attn_b{n}"])[turn])
    d["l0_bv"], d["l0_bo"], d["l0_wo"] = rows(i["L0_attn_bv"]), rows(i["L0_attn_bo"]), t(i["L0_attn_wo"])
    d["l0_gamma"], d["l0_beta"], d["l0_rw"] = col(i["L0_ffn_ln_gamma"]), col(i["L0_ffn_ln_beta"]), t(i["L0_ffn_router_w"])
    d["l0_gate_up"] = np.ascontiguousarray(np.asarray(i["L0_ffn_gate_up_w"]).transpose(0, 2, 1))
    d["l0_down"] = np.ascontiguousarray(np.asarray(i["L0_ffn_down_w"]).transpose(0, 2, 1))
    d["l0_sgu"], d["l0_sd"] = t(i["L0_ffn_shared_gate_up_w"]), t(i["L0_ffn_shared_down_w"])
    d["l1_gamma"] = col(i["L1_attn_gamma"])
    w = np.asarray(i["L1_attn_w_qkv"]).reshape(3, BIG_HEADS, BIG_HD, P)
    d["l1_wqk"] = np.ascontiguousarray(w[:2].transpose(3, 1, 0, 2).reshape(P, -1))
    d["l1_big_wv"] = np.ascontiguousarray(w[2].transpose(2, 0, 1).reshape(P, -1))
    d["l1_wout"] = t(i["L1_attn_w_out"])
    for n in ("ln1_w", "ln1_b", "ln2_w", "ln2_b"):
        d["l1_" + n] = col(i["L1_ffn_" + n])
    d["l1_conv"] = np.ascontiguousarray(np.asarray(i["L1_ffn_conv_w"]).reshape(P, 3))
    aw = np.asarray(i["L1_ffn_attn_w"])
    for n, k in zip("qkv", range(3)):
        d[f"l1_w{n}"] = np.ascontiguousarray(aw[:, k * P:(k + 1) * P])
    for n, k in zip("qk", range(2)):
        d[f"l1_w{n}r"] = np.ascontiguousarray(aw[:, k * P:(k + 1) * P][:, turn])
    d["l1_proj"], d["l1_rw"] = np.ascontiguousarray(i["L1_ffn_proj_w"]), np.ascontiguousarray(i["L1_ffn_router_w"])
    d["l1_gate_up"], d["l1_down"] = np.ascontiguousarray(i["L1_ffn_expert_wv"]), np.ascontiguousarray(i["L1_ffn_expert_proj"])
    return d


def kernel(**inputs):
    import numpy as np
    import concourse.bacc as bacc
    from concourse.bass_utils import run_bass_kernel_spmd

    nc = bacc.Bacc("TRN2", target_bir_lowering=False, num_devices=1)
    arrays = {f"in_{n}": v for n, v in {**layouts(inputs), **constants()}.items()}
    aps = {n[3:]: nc.dram_tensor(n, v.shape, mybir.dt.from_np(v.dtype), kind="ExternalInput").ap()
           for n, v in arrays.items()}
    out = nc.dram_tensor("out_tokens", (T, P), F32, kind="ExternalOutput").ap()
    two_layers(nc, aps, out)
    r = run_bass_kernel_spmd(nc, [arrays], core_ids=[0])
    return np.asarray(r.results[0]["out_tokens"]).reshape(1, T, P)
```

```python
from contextlib import ExitStack

import concourse.bass as bass
from concourse import mybir

F32 = mybir.dt.float32
BF16 = mybir.dt.bfloat16
ALU = mybir.AluOpType
ACT = mybir.ActivationFunctionType
AX = mybir.AxisListType

P = 128
T = 2048
NT = T // P
BLK = 512
NB = T // BLK
TPB = BLK // P
HEADS, HD = 16, 8
NPACK = 4
HPP = HEADS // NPACK
TERMS = 3
PROD = TERMS * TERMS * HD
SHIFT0 = PROD
ROWS = PROD + TERMS
LN_EPS = 1e-5
BIG_HEADS, BIG_HD = 8, 128
NEG = -3.0e38
START = 1


def is_first(block):
    return isinstance(block, int) and block == 0


class Core:

    def __init__(self, nc, stack):
        self.nc, self.used = nc, []
        self.psum = stack.enter_context(nc.psum_tensor("psum", [P, 8, BLK], F32))

    def sb(self, stack, name, shape, dt=F32):
        return stack.enter_context(self.nc.sbuf_tensor(name, shape, dt))

    def sem(self, stack, name):
        self.used.append(self.nc.alloc_semaphore(name))
        return self.used[-1]

    def recycle_semaphores(self):
        self.nc.clear_and_free_semaphores(self.used)
        self.nc.all_engine_barrier()
        self.used = []


def start_counts(eng, *sems):
    for s in sems:
        eng.sem_inc(s, START)


class Chain:

    def __init__(self, eng, sem):
        self.eng, self.sem, self.n = eng, sem, 0

    def link(self, ins):
        self.n += 1
        ins.then_inc(self.sem, 1)

    def settle(self):
        self.eng.wait_ge(self.sem, self.n)


def layer_norm(eng, chain, x, out, st, var_ready, rstd_ready, tiles):
    stats, mv, veps, rstd = st
    for t in tiles:
        chain.link(eng.bn_stats(stats[:, t, :], x[:, t, :]))
    chain.settle()
    for t in tiles:
        chain.link(eng.bn_aggr(mv[:, t, :], stats[:, t, :]))
    chain.settle()
    eng.tensor_scalar(veps[:, :], mv[:, :, 1], LN_EPS, None, ALU.add).then_inc(var_ready[0], 1)
    eng.wait_ge(rstd_ready[0], rstd_ready[1])
    for t in tiles:
        chain.link(eng.tensor_scalar(out[:, t, :], x[:, t, :], mv[:, t, 0:1], rstd[:, t:t + 1],
                                     ALU.subtract, ALU.mult))
    chain.settle()


def rsqrt_pool(eng, st, half, var_ready, rstd_ready, n):
    eng.wait_ge(var_ready, n)
    eng.tensor_tensor(st[3][:, :], st[2][:, :], half[:, :], ALU.pow).then_inc(rstd_ready, 1)


def small_head_projections(core, tag, src_T, dram, KS, QS, V, biased, table, scratch):
    nc, ps = core.nc, core.psum
    with ExitStack() as st:
        sem = lambda n: core.sem(st, f"{tag}_{n}")
        sb = lambda n, s, dt=F32: core.sb(st, f"{tag}_{n}", s, dt)
        w = {n: sb(n, [P, P]) for n in ("wq", "wqr", "wk", "wkr", "wv")}
        b = {n: sb(n, [P, 1]) for n in ("bq", "bqr", "bk", "bkr")} if biased else {}
        bv = sb("bv", [P, P]) if biased else None
        cs = sb("cs", [P, 2, 2, BLK])
        t1, t2 = sb("t1", [P, 2, BLK]), sb("t2", [P, 2, BLK])
        terms = sb("terms", [P, 2, TERMS, BLK], BF16)
        w_in, cs_in = sem("w_in"), [sem("cs_in0"), sem("cs_in1")]
        qk_ready, qk_read = sem("qk_ready"), sem("qk_read")
        v_ready, v_read = sem("v_ready"), sem("v_read")
        rot, hi, rest, mid, low = (sem(n) for n in ("rot", "hi", "rest", "mid", "low"))
        half_done, ones_set = sem("half_done"), sem("ones_set")
        stored, stacked = sem("stored"), [sem("stacked0"), sem("stacked1")]
        steps = [("k", n) for n in range(NB)] + [("q", n) for n in range(NB)]
        NS = len(steps)

        def loads_before(s):
            return sum(16 * TERMS * (1 if which == "k" else TERMS)
                       for which, _ in steps[s % 2:min(s, NS):2])
        with nc.Block() as block:
            @block.sync
            def _(sp):
                for n in w:
                    sp.dma_start(w[n][:, :], dram[n]).then_inc(w_in, 16)
                for n in b:
                    sp.dma_start(b[n][:, :], dram[n]).then_inc(w_in, 16)
                if biased:
                    sp.dma_start(bv[:, :], dram["bv"]).then_inc(w_in, 16)

                def stack_terms(s):
                    which, n = steps[s]
                    sp.wait_ge(stored, 16 * TERMS * (s + 1))
                    dst = QS if which == "q" else KS
                    group = TERMS * HD
                    for g in range(TERMS):
                        if which == "k":
                            sp.dma_start(dst[g * group:(g + 1) * group, :, n * BLK:(n + 1) * BLK],
                                         scratch[s % 2].rearrange("h t d n -> (t d) h n")).then_inc(stacked[s % 2], 16)
                            continue
                        for r in range(TERMS):
                            row = g * group + r * HD
                            sp.dma_start(dst[row:row + HD, :, n * BLK:(n + 1) * BLK],
                                         scratch[s % 2, :, g].rearrange("h d n -> d h n")).then_inc(stacked[s % 2], 16)

                def store(s):
                    for t in range(TERMS):
                        sp.dma_start(scratch[s % 2, :, t], terms[:, s % 2, t, :]).then_inc(stored, 16)

                for s, (which, n) in enumerate(steps):
                    if s >= 1:
                        if s >= 3:
                            sp.wait_ge(stacked[(s - 1) % 2], loads_before(s - 1))
                        sp.wait_ge(low, s)
                        store(s - 1)
                        if s == 1:
                            sp.wait_ge(half_done, 2)
                        stack_terms(s - 1)
                sp.wait_ge(low, NS)
                sp.wait_ge(stacked[(NS - 1) % 2], loads_before(NS - 1))
                store(NS - 1)
                stack_terms(NS - 1)
                for s in (NS, NS + 1):
                    sp.wait_ge(stacked[s % 2], loads_before(s))

            @block.gpsimd
            def _(pool):
                pool.memset(KS[64:ROWS, 0:HEADS // 2, :], -1.0).then_inc(half_done, 1)
                pool.wait_ge(half_done, 1)
                pool.memset(KS[64:ROWS, HEADS // 2:, :], -1.0).then_inc(half_done, 1)
                pool.wait_ge(half_done, 2)
                pool.memset(V[:, :, :, HD:], 1.0).then_inc(ones_set, 1)

            @block.tensor
            def _(pe):
                pe.wait_ge(w_in, 16 * (len(w) + len(b) + bool(biased)))
                for s, (which, n) in enumerate(steps):
                    if s >= 2:
                        pe.wait_ge(qk_read, s - 1)
                    cols = src_T[:, n * BLK:(n + 1) * BLK]
                    pe.matmul(ps[:, 2 * (s % 2), :], w["w" + which][:, :], cols, start=True, stop=True)
                    pe.matmul(ps[:, 2 * (s % 2) + 1, :], w["w" + which + "r"][:, :], cols,
                              start=True, stop=True).then_inc(qk_ready, 1)
                for g in range(NB):
                    if g >= 2:
                        pe.wait_ge(v_read, TPB * (g - 1))
                    for i in range(TPB):
                        t = g * TPB + i
                        mm = pe.matmul(ps[:, 4 + g % 2, i * P:(i + 1) * P], src_T[:, t * P:(t + 1) * P],
                                       w["wv"][:, :], start=True, stop=True)
                    mm.then_inc(v_ready, 1)

            @block.scalar
            def _(act):
                def load_table(s):
                    n = steps[s][1]
                    act.dma_start(cs[:, s % 2, :, :], table[:, :, n * BLK:(n + 1) * BLK]).then_inc(cs_in[s % 2], 16)
                load_table(0)
                load_table(1)
                for s in range(NS):
                    act.wait_ge(rot, s + 1)
                    if s + 2 < NS:
                        load_table(s + 2)
                    if s >= 2:
                        act.wait_ge(stored, 16 * TERMS * (s - 1))
                    act.activation(terms[:, s % 2, 0, :], t1[:, s % 2, :], ACT.Copy).then_inc(hi, 1)
                    act.wait_ge(rest, s + 1)
                    act.activation(terms[:, s % 2, 1, :], t2[:, s % 2, :], ACT.Copy).then_inc(mid, 1)

            @block.vector
            def _(dve):
                part = Chain(dve, sem("part"))
                dve.wait_ge(w_in, 16 * (len(w) + len(b) + bool(biased)))

                def split(s):
                    u = s % 2
                    dve.wait_ge(hi, s + 1)
                    dve.tensor_tensor(t2[:, u, :], t1[:, u, :], terms[:, u, 0, :], ALU.subtract).then_inc(rest, 1)
                    dve.wait_ge(mid, s + 1)
                    dve.tensor_tensor(terms[:, u, 2, :], t2[:, u, :], terms[:, u, 1, :],
                                      ALU.subtract).then_inc(low, 1)

                for s, (which, n) in enumerate(steps):
                    u = s % 2
                    dve.wait_ge(cs_in[u], 16 * (s // 2 + 1))
                    dve.wait_ge(qk_ready, s + 1)
                    if s >= 2:
                        dve.wait_ge(low, s - 1)
                    for j, (t, name) in enumerate(((t1, "b" + which), (t2, "b" + which + "r"))):
                        src = ps[:, 2 * u + j, :]
                        if biased:
                            ins = dve.scalar_tensor_tensor(out=t[:, u, :], in0=src, scalar=b[name][:, 0:1],
                                                           in1=cs[:, u, j, :], op0=ALU.add, op1=ALU.mult)
                        else:
                            ins = dve.tensor_tensor(t[:, u, :], src, cs[:, u, j, :], ALU.mult)
                        part.link(ins)
                    part.settle()
                    dve.tensor_tensor(t1[:, u, :], t1[:, u, :], t2[:, u, :], ALU.add).then_inc(rot, 1)
                    dve.sem_inc(qk_read, 1)
                    if s >= 1:
                        split(s - 1)
                split(NS - 1)
                dve.wait_ge(ones_set, 1)
                for t in range(NT):
                    g, i = t // TPB, t % TPB
                    dve.wait_ge(v_ready, g + 1)
                    src = ps[:, 4 + g % 2, i * P:(i + 1) * P].rearrange("p (h d) -> p h d", d=HD)
                    if biased:
                        ins = dve.tensor_tensor(V[:, t, :, 0:HD], src,
                                                bv[:, :].rearrange("p (h d) -> p h d", d=HD), ALU.add)
                    else:
                        ins = dve.tensor_copy(V[:, t, :, 0:HD], src)
                    ins.then_inc(v_read, 1)


MAX_W = 2 * BLK
S_BANK, S_SLOTS = 4, 3
AV_BANK = 7
P_SLOTS = 8
LEAD = 2


def small_head_attention(core, tag, KS, QS, V, OT, sel, sel_dram, diag_neg, causal):
    nc, ps = core.nc, core.psum
    scale = float(HD) ** -0.5

    def key_tiles(qb):
        return TPB * (qb + 1) if causal else NT

    def units(qb):
        out = []
        for p in range(NPACK):
            mine = []
            for j in range(HPP):
                for qt in range(TPB):
                    keys = (TPB * qb + qt + 1) * P if causal else T
                    for u in range(-(-keys // MAX_W)):
                        mine.append(("scores", 0, p, j, qt, u, min(MAX_W, keys - u * MAX_W)))
            out.append(mine)
        return out

    def items(qb, p):
        if qb is None:
            first, second = units(0)[:LEAD]
            return first + second[:2] + [("turn", 0, 0)] + second[2:]
        off, t = divmod(p + LEAD, NPACK)
        turn = [("turn", (p + 1) // NPACK, (p + 1) % NPACK)]
        if off and qb == NB - 1:
            return turn if p + 1 < NPACK else []
        us = [(kind, off, *rest) for kind, _, *rest in units(qb + off)[t]]
        return us[:2] + turn + us[2:]

    def parts(qb):
        return -(-((TPB * (qb + 1)) * P if causal else T) // MAX_W)

    n_items = [sum(len(items(q, p)) for p in range(NPACK)) for q in range(NB)]
    n_ahead = len(items(None, 0))
    n_exp = [HEADS * key_tiles(q) for q in range(NB)]
    n_step = [NPACK * key_tiles(q) for q in range(NB)]

    def before(counts, qb):
        return sum(counts[:qb]) if isinstance(qb, int) else qb * counts[0]

    with ExitStack() as st:
        sem = lambda n: core.sem(st, f"{tag}_{n}")
        sb = lambda n, s, dt=F32: core.sb(st, f"{tag}_{n}", s, dt)
        probs = sb("probs", [P, P_SLOTS, BLK])
        OD = sb("OD", [P, NPACK, BLK])
        rden = sb("rden", [P, BLK])
        mx = sb("mx", [P, 2, TPB, HPP, 2])
        mxr = sb("mxr", [P, 2, TPB, HPP])
        mrow = sb("mrow", [HPP, 2, BLK])
        mrest = sb("mrest", [HPP, BLK])
        zero4 = sb("zero4", [HPP, BLK])
        mterm = sb("mterm", [HPP, 2, TERMS, BLK], BF16)
        sel_in, bank_zeroed, zero_set = sem("sel_in"), sem("bank_zeroed"), sem("zero_set")
        max_ready, max_read, mx_ready = sem("max_ready"), sem("max_read"), sem("mx_ready")
        masked_neg, row_ready = sem("masked_neg"), sem("row_ready")
        split_step, split_done, shift_in = sem("split_step"), sem("split_done"), [sem(f"shift_in{p}") for p in range(NPACK)]
        s_ready, exp_done, masked, av_done = sem("s_ready"), sem("exp_done"), sem("masked"), sem("av_done")
        od_done, sel_ready, sel_rden, sel_read = sem("od_done"), sem("sel_ready"), sem("sel_rden"), sem("sel_read")

        def q_cols(qb, a, n):
            return slice(qb * BLK + a, qb * BLK + a + n) if isinstance(qb, int) else bass.ds(qb * BLK + a, n)

        def first_col(qb, kt):
            return P * max(0, kt - TPB * qb) if causal else 0

        def blocks(eng, body):
            body(None)
            if causal:
                for qb in range(NB - 1):
                    body(qb)
            else:
                with eng.Fori(0, NB - 1) as qb:
                    body(qb)
            body(NB - 1)

        def shape_of(qb):
            return qb if isinstance(qb, int) else 0

        def item_rows(qb):
            if qb is None:
                return [[(k, k % 2, 0, item) for k, item in enumerate(items(None, 0))]]
            rows, k = [], 0
            for p in range(NPACK):
                rows.append([])
                for item in items(shape_of(qb), p):
                    n = n_ahead + before(n_items, qb) + k
                    slot = (n_ahead + before(n_items, shape_of(qb)) + k) % 2
                    rows[-1].append((n, slot, qb + item[1], item))
                    k += 1
            return rows

        with nc.Block() as block:
            @block.sync
            def _(sp):
                sp.dma_start(sel[:, :, :, :], sel_dram).then_inc(sel_in, 16)

                def body(qb):
                    for row in item_rows(qb):
                        for _, _, of, item in row:
                            if item[0] != "turn":
                                continue
                            p = item[2]
                            sp.wait_ge(split_done, NPACK * of + p + 1)
                            for j in range(HPP):
                                sp.dma_start(QS[SHIFT0:ROWS, HPP * p + j, q_cols(of, 0, BLK)],
                                             mterm[j:j + 1, p % 2, :, :]).then_inc(shift_in[p], 16)
                blocks(sp, body)
                for p in range(NPACK):
                    sp.wait_ge(shift_in[p], 16 * HPP * NB)

            @block.gpsimd
            def _(pool):
                pool.memset(zero4[:, :], 0.0).then_inc(zero_set, 1)
                pool.wait_ge(zero_set, 1)

                def split(nxt, p):
                    n = NPACK * nxt + p
                    u = p % 2
                    if p >= 2:
                        pool.wait_ge(shift_in[p - 2], 16 * HPP * (nxt + 1))
                    elif not is_first(nxt):
                        pool.wait_ge(shift_in[p + 2], 16 * HPP * nxt)
                    pool.wait_ge(row_ready, n + 1)
                    pool.tensor_tensor(mterm[:, u, 0, :], mrow[:, u, :], zero4[:, :], ALU.add).then_inc(split_step, 1)
                    pool.wait_ge(split_step, 3 * n + 1)
                    pool.tensor_tensor(mrest[:, :], mrow[:, u, :], mterm[:, u, 0, :], ALU.subtract).then_inc(split_step, 1)
                    pool.wait_ge(split_step, 3 * n + 2)
                    pool.tensor_tensor(mterm[:, u, 1, :], mrest[:, :], zero4[:, :], ALU.add).then_inc(split_step, 1)
                    pool.wait_ge(split_step, 3 * n + 3)
                    pool.tensor_tensor(mterm[:, u, 2, :], mrest[:, :], mterm[:, u, 1, :],
                                       ALU.subtract).then_inc(split_done, 1)

                def body(qb):
                    for p, row in enumerate(item_rows(qb)):
                        for _, _, of, item in row:
                            if item[0] == "turn":
                                split(of, item[2])
                        if qb is None or not causal:
                            continue
                        for kt in range(TPB * qb, TPB * (qb + 1)):
                            for j in range(HPP):
                                e = HPP * (p * key_tiles(qb) + kt) + j
                                c = first_col(qb, kt)
                                tile = probs[:, e % P_SLOTS, c:c + P]
                                pool.wait_ge(exp_done, START + before(n_exp, qb) + e + 1)
                                pool.affine_select(out=tile, in_=tile, compare_op=ALU.is_ge, fill=0.0,
                                                   base=0, pattern=[[1, P]],
                                                   channel_multiplier=-1).then_inc(masked, 1)
                blocks(pool, body)

            @block.tensor
            def _(pe):
                start_counts(pe, av_done, sel_ready)
                pe.wait_ge(sel_in, 16)
                pe.wait_ge(bank_zeroed, 1)

                def max_item(n, slot, nxt, item):
                    if not isinstance(n, int) or n >= 2:
                        pe.wait_ge(max_read, n - 1)
                    if item[0] == "turn":
                        p = item[2]
                        pe.wait_ge(mx_ready, NPACK * nxt + p + 1)
                        for qt in range(TPB):
                            mm = pe.transpose(ps[0:HPP, 2 * slot, qt * P:(qt + 1) * P], mxr[:, p % 2, qt, :],
                                              core.ident[:, :])
                        mm.then_inc(max_ready, 1)
                        return
                    _, _, p, j, qt, u, width = item
                    h = HPP * p + j
                    for a in range(0, width, BLK):
                        w = min(BLK, width - a)
                        k0 = u * MAX_W + a
                        mm = pe.matmul(ps[:, 2 * slot + a // BLK, 0:w], QS[0:PROD, h, q_cols(nxt, qt * P, P)],
                                       KS[0:PROD, h, k0:k0 + w], start=True, stop=True)
                    mm.then_inc(max_ready, 1)

                def body(qb):
                    rows = item_rows(qb)
                    if qb is None:
                        for what in rows[0]:
                            max_item(*what)
                        return
                    K = key_tiles(shape_of(qb))
                    steps = NPACK * K
                    e0, s0 = before(n_exp, qb), before(n_step, qb)
                    m0 = before([TPB * HEADS] * NB, qb)

                    def av(s):
                        p, kt = s // K, s % K
                        c = first_col(qb, kt)
                        if kt == 0:
                            pe.wait_ge(od_done, START + NPACK * qb + p)
                        if causal and kt >= TPB * qb:
                            pe.wait_ge(masked, m0 + HPP * (p * TPB + kt - TPB * qb) + HPP)
                        else:
                            pe.wait_ge(exp_done, START + e0 + HPP * s + HPP)
                        for j in range(HPP):
                            e = HPP * s + j
                            mm = pe.matmul(ps[32 * j:32 * j + 2 * HD, AV_BANK, c:BLK], V[:, kt, HPP * p + j, :],
                                           probs[:, e % P_SLOTS, c:BLK], start=(kt == 0), stop=(kt == K - 1),
                                           skip_group_check=True)
                        mm.then_inc(av_done, 1)

                    for s in range(steps):
                        p, kt = s // K, s % K
                        c = first_col(qb, kt)
                        if kt == 0:
                            done = 0
                        for j in range(HPP):
                            e = HPP * s + j
                            if kt == 0 and j == 0:
                                pe.wait_ge(shift_in[p], 16 * HPP * (qb + 1))
                            if e == 0:
                                pe.wait_ge(sel_read, START + qb)
                            pe.wait_ge(exp_done, START + e0 + max(e - S_SLOTS + 1, 0))
                            h = HPP * p + j
                            pe.matmul(ps[:, S_BANK + e % S_SLOTS, c:BLK], KS[0:ROWS, h, kt * P:(kt + 1) * P],
                                      QS[0:ROWS, h, q_cols(qb, c, BLK - c)], start=True, stop=True).then_inc(s_ready, 1)
                            if j % 2:
                                upto = -(-len(rows[p]) * (2 * kt + 1 + j // 2) // (2 * K))
                                for what in rows[p][done:upto]:
                                    max_item(*what)
                                done = upto
                        if s >= 1:
                            av(s - 1)
                    av(steps - 1)
                    pe.wait_ge(od_done, START + NPACK * qb + NPACK)
                    for which in range(2):
                        for p in range(NPACK):
                            mm = pe.matmul(ps[:, S_BANK + which, :], sel[:, which, p, :], OD[:, p, :],
                                           start=(p == 0), stop=(p == NPACK - 1))
                    mm.then_inc(sel_ready, 1)
                blocks(pe, body)

            @block.scalar
            def _(act):
                start_counts(act, exp_done, od_done)

                def body(qb):
                    if qb is None:
                        return
                    K = key_tiles(shape_of(qb))
                    steps = NPACK * K
                    e0, s0 = before(n_exp, qb), before(n_step, qb)

                    def od_copy(p):
                        act.wait_ge(av_done, START + s0 + K * (p + 1))
                        if p == 0:
                            act.wait_ge(sel_ready, START + qb)
                        act.activation(OD[:, p, :], ps[:, AV_BANK, :], ACT.Copy).then_inc(od_done, 1)

                    for s in range(steps):
                        p, kt = s // K, s % K
                        c = first_col(qb, kt)
                        for j in range(HPP):
                            e = HPP * s + j
                            act.wait_ge(s_ready, e0 + e + 1)
                            if j == 0:
                                act.wait_ge(av_done, START + s0 + max(s - 1, 0))
                            act.activation(probs[:, e % P_SLOTS, c:BLK], ps[:, S_BANK + e % S_SLOTS, c:BLK],
                                           ACT.Exp, scale=scale).then_inc(exp_done, 1)
                        if kt == 0 and p >= 1:
                            od_copy(p - 1)
                    od_copy(NPACK - 1)
                blocks(act, body)

            @block.vector
            def _(dve):
                start_counts(dve, sel_read)
                dve.memset(ps[:, AV_BANK, :], 0.0).then_inc(bank_zeroed, 1)

                def max_item(n, slot, nxt, item, neg):
                    dve.wait_ge(max_ready, n + 1)
                    if item[0] == "turn":
                        p = item[2]
                        r = NPACK * nxt + p
                        if not is_first(nxt) or p >= 2:
                            dve.wait_ge(split_done, r - 1)
                        dve.tensor_copy(mrow[:, p % 2, :], ps[0:HPP, 2 * slot, :]).then_inc(row_ready, 1)
                        dve.wait_ge(row_ready, r + 1)
                        dve.sem_inc(max_read, 1)
                        return neg
                    _, _, p, j, qt, u, width = item
                    banks = ps[:, 2 * slot:2 * slot + 2, :].rearrange("p b n -> p (b n)")
                    if causal and u == parts(nxt) - 1:
                        diag = banks[:, width - P:width]
                        neg += 1
                        dve.tensor_tensor(diag, diag, diag_neg[:, :], ALU.add).then_inc(masked_neg, 1)
                        dve.wait_ge(masked_neg, neg)
                    dve.tensor_reduce(mx[:, p % 2, qt, j, u:u + 1], banks[:, 0:width], AX.X,
                                      ALU.max).then_inc(max_read, 1)
                    if (j, qt, u) == (HPP - 1, TPB - 1, parts(shape_of(nxt)) - 1):
                        dve.wait_ge(max_read, n + 1)
                        dve.tensor_reduce(mxr[:, p % 2, :, :], mx[:, p % 2, :, :, 0:parts(shape_of(nxt))],
                                          AX.X, ALU.max).then_inc(mx_ready, 1)
                    return neg

                state = [0]

                def body(qb):
                    for row in item_rows(qb):
                        for what in row:
                            state[0] = max_item(*what, state[0])
                    if qb is not None:
                        dve.wait_ge(sel_ready, START + qb + 1)
                        dve.reciprocal(rden[:, :], ps[:, S_BANK + 1, :]).then_inc(sel_rden, 1)
                        dve.wait_ge(sel_rden, qb + 1)
                        dve.tensor_tensor(OT[:, q_cols(qb, 0, BLK)], ps[:, S_BANK, :], rden[:, :],
                                          ALU.mult).then_inc(sel_read, 1)
                blocks(dve, body)


def routing(dve, act_pair, chain, lg, prob, cand, pick, comb, rank, small, n_exp, top2):
    E = rank.shape[2]
    e_in, e_out = act_pair
    m, r, v2, g1, g2 = (small[:, i, :] for i in range(5))

    def wide(v):
        return v.unsqueeze(2).broadcast_to([P, NT, E])

    def step(ins):
        chain.link(ins)
        chain.settle()

    def first_of(values, top, out):
        step(dve.tensor_tensor(cand[:, :, :], values, wide(top), ALU.is_equal))
        step(dve.tensor_tensor(cand[:, :, :], cand[:, :, :], rank[:, :, :], ALU.mult))
        step(dve.tensor_reduce(v2, cand[:, :, :], AX.X, ALU.max))
        step(dve.tensor_tensor(out, rank[:, :, :], wide(v2), ALU.is_equal))

    step(dve.tensor_reduce(m, lg, AX.X, ALU.max))
    if not top2:
        first_of(lg, m, comb)
        return
    step(dve.tensor_tensor(prob[:, :, :], lg, wide(m), ALU.subtract))
    dve.sem_inc(e_in, 1)
    dve.wait_ge(e_out, 1)
    step(dve.tensor_reduce(r, prob[:, :, :], AX.X, ALU.add))
    step(dve.reciprocal(r, r))
    step(dve.tensor_tensor(prob[:, :, :], prob[:, :, :], wide(r), ALU.mult))
    step(dve.tensor_reduce(m, prob[:, :, :], AX.X, ALU.max))
    first_of(prob[:, :, :], m, pick[:, 0])
    step(dve.scalar_tensor_tensor(out=prob[:, :, :], in0=pick[:, 0], scalar=-2.0, in1=prob[:, :, :],
                                  op0=ALU.mult, op1=ALU.add))
    step(dve.tensor_reduce(r, prob[:, :, :], AX.X, ALU.max))
    first_of(prob[:, :, :], r, pick[:, 1])
    step(dve.tensor_tensor(g2, r, m, ALU.subtract))
    dve.sem_inc(e_in, 1)
    dve.wait_ge(e_out, 2)
    step(dve.tensor_scalar(g1, g2, 1.0, None, ALU.add))
    step(dve.reciprocal(g1, g1))
    step(dve.tensor_tensor(g2, g2, g1, ALU.mult))
    step(dve.tensor_tensor(pick[:, 0], pick[:, 0], wide(g1), ALU.mult))
    step(dve.tensor_tensor(pick[:, 1], pick[:, 1], wide(g2), ALU.mult))
    step(dve.tensor_tensor(comb, pick[:, 0], pick[:, 1], ALU.add))


def project_norm_route(core, tag, OT, X, hT, comb, dram, E, post_norm, bias, top2):
    nc, ps = core.nc, core.psum
    with ExitStack() as st:
        sem = lambda n: core.sem(st, f"{tag}_{n}")
        sb = lambda n, s, dt=F32: core.sb(st, f"{tag}_{n}", s, dt)
        wo, gamma, beta, rw = sb("wo", [P, P]), sb("gamma", [P, 1]), sb("beta", [P, 1]), sb("rw", [P, E])
        bo = sb("bo", [P, P]) if bias else None
        rank = sb("rank", [P, NT, E])
        N = sb("N", [P, NT, P])
        stats = (sb("stats", [P, NT, 6]), sb("mv", [P, NT, 2]), sb("veps", [P, NT]), sb("rstd", [P, NT]))
        half = sb("half", [P, NT])
        lg, prob, cand = (sb(n, [P, NT, E]) for n in ("lg", "prob", "cand"))
        pick = sb("pick", [P, 2, NT, E])
        small = sb("small", [P, 5, NT])
        w_in, y_ready, n_ready, turned, h_ready, lg_ready = (
            sem(n) for n in ("w_in", "y_ready", "n_ready", "turned", "h_ready", "lg_ready"))
        var_ready, rstd_ready, half_set, e_in, e_out = (
            sem(n) for n in ("var_ready", "rstd_ready", "half_set", "e_in", "e_out"))
        loads = [(wo[:, :], dram["wo"]), (gamma[:, :], dram["gamma"]), (beta[:, :], dram["beta"]),
                 (rw[:, :], dram["rw"]), (rank[:, :, :], dram["rank"])]
        if bias:
            loads.append((bo[:, :], dram["bo"]))
        with nc.Block() as block:
            @block.sync
            def _(sp):
                for dst, src in loads:
                    sp.dma_start(dst, src).then_inc(w_in, 16)

            @block.gpsimd
            def _(pool):
                pool.memset(half[:, :], -0.5).then_inc(half_set, 1)
                pool.wait_ge(half_set, 1)
                for n in range(1 + bool(post_norm)):
                    rsqrt_pool(pool, stats, half, var_ready, rstd_ready, n + 1)

            @block.tensor
            def _(pe):
                pe.wait_ge(w_in, 16 * len(loads))
                for g in range(NB):
                    for i in range(TPB):
                        t = g * TPB + i
                        mm = pe.matmul(ps[:, g, i * P:(i + 1) * P], OT[:, t * P:(t + 1) * P], wo[:, :],
                                       start=True, stop=True)
                    mm.then_inc(y_ready, 1)
                for g in range(NB):
                    pe.wait_ge(n_ready, 1)
                    for i in range(TPB):
                        t = g * TPB + i
                        mm = pe.transpose(ps[:, 4 + g % 2, i * P:(i + 1) * P], N[:, t, :], core.ident[:, :])
                    mm.then_inc(turned, 1)
                    if g >= 1:
                        pe.wait_ge(h_ready, g)
                pe.wait_ge(h_ready, NB)
                for t in range(NT):
                    mm = pe.matmul(ps[:, 6, t * E:(t + 1) * E], hT[:, t * P:(t + 1) * P], rw[:, :],
                                   start=True, stop=True)
                mm.then_inc(lg_ready, 1)

            @block.scalar
            def _(act):
                if top2:
                    act.wait_ge(e_in, 1)
                    act.activation(prob[:, :, :], prob[:, :, :], ACT.Exp).then_inc(e_out, 1)
                    act.wait_ge(e_in, 2)
                    act.activation(small[:, 4, :], small[:, 4, :], ACT.Exp).then_inc(e_out, 1)

            @block.vector
            def _(dve):
                chain = Chain(dve, sem("chain"))
                dve.wait_ge(w_in, 16 * len(loads))
                for t in range(NT):
                    if bias:
                        chain.link(dve.tensor_tensor(X[:, t, :], X[:, t, :], bo[:, :], ALU.add))
                chain.settle()
                for g in range(NB):
                    dve.wait_ge(y_ready, g + 1)
                    mine = X[:, g * TPB:(g + 1) * TPB, :]
                    chain.link(dve.tensor_tensor(mine, ps[:, g, :].rearrange("p (t c) -> p t c", c=P), mine, ALU.add))
                chain.settle()
                n = 0
                if post_norm:
                    n += 1
                    layer_norm(dve, chain, X, X, stats, (var_ready,), (rstd_ready, n), range(NT))
                n += 1
                layer_norm(dve, chain, X, N, stats, (var_ready,), (rstd_ready, n), range(NT))
                dve.sem_inc(n_ready, 1)
                for g in range(NB):
                    dve.wait_ge(turned, g + 1)
                    dve.tensor_scalar(hT[:, g * BLK:(g + 1) * BLK], ps[:, 4 + g % 2, :], gamma[:, 0:1], beta[:, 0:1],
                                      ALU.mult, ALU.add).then_inc(h_ready, 1)
                dve.wait_ge(lg_ready, 1)
                chain.link(dve.tensor_copy(lg[:, :, :], ps[:, 6, 0:NT * E].rearrange("p (t e) -> p t e", e=E)))
                chain.settle()
                routing(dve, (e_in, e_out), chain, lg[:, :, :], prob, cand, pick, comb[:, :, 0:E], rank, small, 0, top2)
                if top2:
                    chain.link(dve.memset(comb[:, :, E:E + 1], 1.0))
                chain.settle()


def experts(core, tag, hT, comb, acc, gate_up, down, E, NF, shared):
    nc, ps = core.nc, core.psum
    F = NF * P
    with ExitStack() as st:
        sem = lambda n: core.sem(st, f"{tag}_{n}")
        sb = lambda n, s, dt=F32: core.sb(st, f"{tag}_{n}", s, dt)
        wgu = sb("wgu", [P, 2, 2 * F])
        wd = sb("wd", [P, 2, NF, P])
        sgu, sd = (sb("sgu", [P, 2 * P]), sb("sd", [P, P])) if shared else (None, None)
        gate = sb("gate", [P, 2, BLK])
        prod = sb("prod", [P, 2, NF, BLK])
        w_in = [sem("w_in0"), sem("w_in1")]
        s_in = sem("s_in")
        gu_ready, gu_free, silu_done, prod_ready = (sem(n) for n in ("gu_ready", "gu_free", "silu_done", "prod_ready"))
        y_ready, y_free = sem("y_ready"), sem("y_free")
        UNITS = 2 * NB
        PAIRS = E // 2

        with nc.Block() as block:
            @block.sync
            def _(sp):
                def load(slot, e):
                    one = slice(e, e + 1) if isinstance(e, int) else bass.ds(e, 1)
                    sp.dma_start(wgu[:, slot, :], gate_up[one].rearrange("o d f -> (o d) f")).then_inc(w_in[slot], 16)
                    sp.dma_start(wd[:, slot, :, :], down[one].rearrange("o (c p) n -> p (o c) n", p=P)).then_inc(w_in[slot], 16)
                load(0, 0)
                load(1, 1)
                if shared:
                    sp.dma_start(sgu[:, :], shared[0]).then_inc(s_in, 16)
                    sp.dma_start(sd[:, :], shared[1]).then_inc(s_in, 16)
                with sp.Fori(0, PAIRS - 1) as it:
                    for slot in range(2):
                        sp.wait_ge(y_ready, it * UNITS + NB * (slot + 1))
                        load(slot, it * 2 + 2 + slot)

            @block.tensor
            def _(pe):
                def up(wts, nf, n, u, b):
                    for c in range(nf):
                        pe.wait_ge(gu_free, n + c + 1)
                        bank = 2 * ((u * nf + c) % 2)
                        cols = hT[:, b * BLK:(b + 1) * BLK]
                        pe.matmul(ps[:, bank, :], wts[:, c * P:(c + 1) * P], cols, start=True, stop=True)
                        pe.matmul(ps[:, bank + 1, :], wts[:, (nf + c) * P:(nf + c + 1) * P], cols,
                                  start=True, stop=True).then_inc(gu_ready, 1)

                def dn(wts, nf, n, u, m):
                    pe.wait_ge(prod_ready, n + nf)
                    pe.wait_ge(y_free, m + 1)
                    for i in range(TPB):
                        for c in range(nf):
                            mm = pe.matmul(ps[:, 4 + u % 2, i * P:(i + 1) * P], prod[:, u % 2, c, i * P:(i + 1) * P],
                                           wts(c), start=(c == 0), stop=(c == nf - 1))
                    mm.then_inc(y_ready, 1)

                with pe.Fori(0, PAIRS) as it:
                    n0, m0 = it * (UNITS * NF), it * UNITS
                    for u in range(UNITS):
                        slot = u // NB
                        if u % NB == 0:
                            pe.wait_ge(w_in[slot], it * 32 + 32)
                        up(wgu[:, slot, :], NF, n0 + u * NF, u, u % NB)
                        if u >= 1:
                            v = u - 1
                            dn(lambda c: wd[:, v // NB, c, :], NF, n0 + v * NF, v, m0 + v)
                    v = UNITS - 1
                    dn(lambda c: wd[:, v // NB, c, :], NF, n0 + v * NF, v, m0 + v)
                if shared:
                    n0, m0 = PAIRS * UNITS * NF, PAIRS * UNITS
                    pe.wait_ge(s_in, 32)
                    for u in range(NB):
                        up(sgu[:, :], 1, n0 + u, u, u)
                        if u >= 1:
                            dn(lambda c: sd[:, :], 1, n0 + u - 1, u - 1, m0 + u - 1)
                    dn(lambda c: sd[:, :], 1, n0 + NB - 1, NB - 1, m0 + NB - 1)

            @block.scalar
            def _(act):
                def silu(nf, n, u):
                    for c in range(nf):
                        k = (u * nf + c) % 2
                        act.wait_ge(gu_ready, n + c + 1)
                        act.wait_ge(gu_free, n + c + 1)
                        act.activation(gate[:, k, :], ps[:, 2 * k, :], ACT.Silu).then_inc(silu_done, 1)
                with act.Fori(0, PAIRS) as it:
                    for u in range(UNITS):
                        silu(NF, it * (UNITS * NF) + u * NF, u)
                if shared:
                    for u in range(NB):
                        silu(1, PAIRS * UNITS * NF + u, u)

            @block.vector
            def _(dve):
                dve.memset(acc[:, 0:NT // 2, :], 0.0).then_inc(gu_free, 2)
                dve.memset(acc[:, NT // 2:, :], 0.0).then_inc(y_free, 2)

                def mult(nf, n, u):
                    for c in range(nf):
                        k = (u * nf + c) % 2
                        dve.wait_ge(silu_done, n + c + 1)
                        dve.tensor_tensor(prod[:, u % 2, c, :], gate[:, k, :], ps[:, 2 * k + 1, :],
                                          ALU.mult).then_inc(prod_ready, 1)
                        dve.wait_ge(prod_ready, n + c + 1)
                        dve.sem_inc(gu_free, 1)

                def gather(m, u, b, e):
                    dve.wait_ge(y_ready, m + 1)
                    one = slice(e, e + 1) if isinstance(e, int) else bass.ds(e, 1)
                    for i in range(TPB):
                        t = b * TPB + i
                        ins = dve.scalar_tensor_tensor(out=acc[:, t, :], in0=ps[:, 4 + u % 2, i * P:(i + 1) * P],
                                                       scalar=comb[:, t, one], in1=acc[:, t, :],
                                                       op0=ALU.mult, op1=ALU.add)
                    ins.then_inc(y_free, 1)
                dve.wait_ge(gu_free, 2)
                dve.wait_ge(y_free, 2)
                with dve.Fori(0, PAIRS) as it:
                    for u in range(UNITS):
                        mult(NF, it * (UNITS * NF) + u * NF, u)
                        if u >= 1:
                            gather(it * UNITS + u - 1, u - 1, (u - 1) % NB, it * 2 + (u - 1) // NB)
                    u = UNITS - 1
                    gather(it * UNITS + u, u, u % NB, it * 2 + u // NB)
                if shared:
                    for u in range(NB):
                        mult(1, PAIRS * UNITS * NF + u, u)
                        if u >= 1:
                            gather(PAIRS * UNITS + u - 1, u - 1, u - 1, E)
                    gather(PAIRS * UNITS + NB - 1, NB - 1, NB - 1, E)


def norm_l2_norm(core, tag, X, acc, xnT, dram):
    nc, ps = core.nc, core.psum
    with ExitStack() as st:
        sem = lambda n: core.sem(st, f"{tag}_{n}")
        sb = lambda n, s, dt=F32: core.sb(st, f"{tag}_{n}", s, dt)
        gamma = sb("gamma", [P, 1])
        stats = (sb("stats", [P, NT, 6]), sb("mv", [P, NT, 2]), sb("veps", [P, NT]), sb("rstd", [P, NT]))
        half = sb("half", [P, 2, NT])
        N = sb("N", [P, NT, P])
        sq, inv = sb("sq", [P, NT]), sb("inv", [P, NT])
        g_in, var_ready, rstd_ready, half_set = (sem(n) for n in ("g_in", "var_ready", "rstd_ready", "half_set"))
        sq_ready, root_ready, n_ready, turned, h_ready = (
            sem(n) for n in ("sq_ready", "root_ready", "n_ready", "turned", "h_ready"))
        with nc.Block() as block:
            @block.sync
            def _(sp):
                sp.dma_start(gamma[:, :], dram["gamma"]).then_inc(g_in, 16)

            @block.gpsimd
            def _(pool):
                pool.memset(half[:, 0, :], -0.5).then_inc(half_set, 1)
                pool.wait_ge(half_set, 1)
                pool.memset(half[:, 1, :], 0.5).then_inc(half_set, 1)
                pool.wait_ge(half_set, 2)
                rsqrt_pool(pool, stats, half[:, 0, :], var_ready, rstd_ready, 1)
                pool.wait_ge(sq_ready, 1)
                pool.tensor_tensor(inv[:, :], sq[:, :], half[:, 1, :], ALU.pow).then_inc(root_ready, 1)

            @block.tensor
            def _(pe):
                pe.wait_ge(n_ready, 1)
                for g in range(NB):
                    for i in range(TPB):
                        mm = pe.transpose(ps[:, g, i * P:(i + 1) * P], N[:, g * TPB + i, :], core.ident[:, :])
                    mm.then_inc(turned, 1)

            @block.vector
            def _(dve):
                chain = Chain(dve, sem("chain"))
                for g in range(NB):
                    mine = slice(g * TPB, (g + 1) * TPB)
                    chain.link(dve.tensor_tensor(X[:, mine, :], X[:, mine, :], acc[:, mine, :], ALU.add))
                chain.settle()
                layer_norm(dve, chain, X, X, stats, (var_ready,), (rstd_ready, 1), range(NT))
                chain.link(dve.tensor_tensor(N[:, :, :], X[:, :, :], X[:, :, :], ALU.mult))
                chain.settle()
                dve.tensor_reduce(sq[:, :], N[:, :, :], AX.X, ALU.add).then_inc(sq_ready, 1)
                dve.wait_ge(root_ready, 1)
                chain.link(dve.tensor_scalar(inv[:, :], inv[:, :], 1e-12, None, ALU.max))
                chain.settle()
                chain.link(dve.reciprocal(inv[:, :], inv[:, :]))
                chain.settle()
                for t in range(NT):
                    chain.link(dve.tensor_scalar(N[:, t, :], X[:, t, :], inv[:, t:t + 1], float(P) ** 0.5,
                                                 ALU.mult, ALU.mult))
                chain.settle()
                dve.sem_inc(n_ready, 1)
                dve.wait_ge(g_in, 16)
                for g in range(NB):
                    dve.wait_ge(turned, g + 1)
                    dve.tensor_scalar(xnT[:, g * BLK:(g + 1) * BLK], ps[:, g, :], gamma[:, 0:1], None,
                                      ALU.mult).then_inc(h_ready, 1)


def big_head_values(core, tag, xnT, V, wv_dram):
    nc, ps = core.nc, core.psum
    W = BIG_HEADS * BIG_HD
    with ExitStack() as st:
        wv = core.sb(st, f"{tag}_wv", [P, W])
        w_in, v_ready, va_read, vd_read = (core.sem(st, f"{tag}_{n}") for n in ("w_in", "v_ready", "va_read", "vd_read"))
        jobs = [(t, c) for t in range(NT) for c in range(W // BLK)]
        with nc.Block() as block:
            @block.sync
            def _(sp):
                sp.dma_start(wv[:, :], wv_dram).then_inc(w_in, 16)

            @block.tensor
            def _(pe):
                pe.wait_ge(w_in, 16)
                for n, (t, c) in enumerate(jobs):
                    if n >= 4:
                        pe.wait_ge(vd_read if n % 2 == 0 else va_read, n // 2 - 1)
                    pe.matmul(ps[:, n % 4, :], xnT[:, t * P:(t + 1) * P], wv[:, c * BLK:(c + 1) * BLK],
                              start=True, stop=True).then_inc(v_ready, 1)

            @block.vector
            def _(dve):
                for n, (t, c) in list(enumerate(jobs))[0::2]:
                    dve.wait_ge(v_ready, n + 1)
                    dve.tensor_copy(V[:, t, c * BLK:(c + 1) * BLK], ps[:, n % 4, :]).then_inc(vd_read, 1)

            @block.scalar
            def _(act):
                for n, (t, c) in list(enumerate(jobs))[1::2]:
                    act.wait_ge(v_ready, n + 1)
                    act.activation(V[:, t, c * BLK:(c + 1) * BLK], ps[:, n % 4, :], ACT.Copy).then_inc(va_read, 1)


def big_head_attention(core, tag, xnT, V, O, wqk_dram, diag_neg):
    nc, ps = core.nc, core.psum
    scale = float(BIG_HD) ** -0.5
    chunks = [(i + TPB) // TPB for i in range(NT)]
    upto = [sum(chunks[:i]) for i in range(NT + 1)]
    NC = upto[-1]
    NPJ = 2 * NB
    PT_SLOTS, T_SLOTS, O_BANK = 4, 3, 7

    def bank0(i):
        return 2 * (i % 2) if chunks[i] <= 2 else 0

    with ExitStack() as st:
        sem = lambda n: core.sem(st, f"{tag}_{n}")
        sb = lambda n, s, dt=F32: core.sb(st, f"{tag}_{n}", s, dt)
        W = sb("W", [P, BIG_HEADS * 2 * BIG_HD])
        wcur = sb("wcur", [P, 2 * BIG_HD])
        KQ = sb("KQ", [P, 2, T])
        probs = sb("probs", [P, 2, T])
        PT = sb("PT", [P, PT_SLOTS, BLK])
        mxc, m = sb("mxc", [P, 4]), sb("m", [P, 1])
        negm, total, rec = sb("negm", [P, 2]), sb("total", [P, 2]), sb("rec", [P, 2])
        w_in, w_cur, pj_ready, k_done, q_done = (sem(n) for n in ("w_in", "w_cur", "pj_ready", "k_done", "q_done"))
        s_ready, neg_done, mx_step, negm_ready, exp_done = (
            sem(n) for n in ("s_ready", "neg_done", "mx_step", "negm_ready", "exp_done"))
        turned, pt_done, av_done, rec_ready, o_done = (
            sem(n) for n in ("turned", "pt_done", "av_done", "rec_ready", "o_done"))
        mx_per_head = NC + sum(c > 1 for c in chunks)

        with nc.Block() as block:
            @block.sync
            def _(sp):
                sp.dma_start(W[:, :], wqk_dram).then_inc(w_in, 16)

            @block.tensor
            def _(pe):
                start_counts(pe, pj_ready, turned, av_done)
                with pe.Fori(0, BIG_HEADS) as h:
                    pe.wait_ge(w_cur, h + 1)
                    pe.wait_ge(exp_done, START + h * NT)
                    pe.wait_ge(pt_done, START + h * NC)

                    def project(n):
                        if n >= 2:
                            pe.wait_ge(k_done if n % 2 == 0 else q_done, h * NB + n // 2)
                        pe.matmul(ps[:, 1 + 2 * (n % 2), :], wcur[:, (1 - n % 2) * P:(2 - n % 2) * P],
                                  xnT[:, (n // 2) * BLK:(n // 2 + 1) * BLK], start=True, stop=True).then_inc(pj_ready, 1)

                    def scores(i):
                        if i >= 1:
                            pe.wait_ge(exp_done, START + h * NT + (max(i - 1, 0) if chunks[i] <= 2 else i))
                        if i == 0 or chunks[i] != chunks[i - 1]:
                            pe.wait_ge(k_done, h * NB + (1 if i == 0 else NB))
                            pe.wait_ge(q_done, h * NB + (1 if i == 0 else NB))
                        for c in range(chunks[i]):
                            w = min(BLK, (i + 1) * P - c * BLK)
                            pe.matmul(ps[:, bank0(i) + c, 0:w], KQ[:, 1, i * P:(i + 1) * P],
                                      KQ[:, 0, c * BLK:c * BLK + w], start=True, stop=True).then_inc(s_ready, 1)

                    def turn(i, c):
                        k = upto[i] + c
                        if c == 0:
                            pe.wait_ge(exp_done, START + h * NT + i + 1)
                        if k >= T_SLOTS:
                            pe.wait_ge(pt_done, START + h * NC + (k - T_SLOTS + 1))
                        for j in range(min(TPB, i + 1 - TPB * c)):
                            kt = TPB * c + j
                            mm = pe.transpose(ps[:, 4 + k % T_SLOTS, j * P:(j + 1) * P],
                                              probs[:, i % 2, kt * P:(kt + 1) * P], core.ident[:, :])
                        mm.then_inc(turned, 1)

                    def product(i, c):
                        k = upto[i] + c
                        pe.wait_ge(pt_done, START + h * NC + (k + 1))
                        if c == 0:
                            pe.wait_ge(o_done, START + h * NT + i)
                        for j in range(min(TPB, i + 1 - TPB * c)):
                            kt = TPB * c + j
                            mm = pe.matmul(ps[:, O_BANK, 0:P], PT[:, k % PT_SLOTS, j * P:(j + 1) * P],
                                           V[:, kt, bass.ds(h * P, P)], start=(kt == 0), stop=(kt == i))
                        mm.then_inc(av_done, 1)

                    project(0)
                    project(1)
                    scores(0)
                    project(2)
                    for i in range(NT):
                        turn(i, 0)
                        if chunks[i] > 1:
                            turn(i, 1)
                        if i == 3:
                            project(6)
                            project(7)
                        if i + 1 < NT:
                            scores(i + 1)
                        if i < 3:
                            project(3 + i)
                        for c in range(chunks[i]):
                            if c >= 1 and c + 1 < chunks[i]:
                                turn(i, c + 1)
                            product(i, c)

            @block.vector
            def _(dve):
                start_counts(dve, pt_done)
                dve.wait_ge(w_in, 16)
                with dve.Fori(0, BIG_HEADS) as h:
                    dve.wait_ge(pj_ready, START + h * NPJ)
                    dve.tensor_copy(wcur[:, :], W[:, bass.ds(h * (2 * P), 2 * P)]).then_inc(w_cur, 1)

                    def keys(n):
                        dve.wait_ge(pj_ready, START + h * NPJ + (n + 1))
                        dve.tensor_copy(KQ[:, 0, (n // 2) * BLK:(n // 2 + 1) * BLK], ps[:, 1, :]).then_inc(k_done, 1)

                    def evac(i, c):
                        k = upto[i] + c
                        w = min(BLK, (i + 1) * P - c * BLK)
                        dve.wait_ge(turned, START + h * NC + (k + 1))
                        dve.wait_ge(av_done, START + h * NC + max(k - PT_SLOTS + 1, 0))
                        dve.tensor_copy(PT[:, k % PT_SLOTS, 0:w], ps[:, 4 + k % T_SLOTS, 0:w]).then_inc(pt_done, 1)

                    def invert(i):
                        dve.wait_ge(o_done, START + h * NT + max(i - 1, 0))
                        dve.wait_ge(exp_done, START + h * NT + (i + 1))
                        dve.reciprocal(rec[:, i % 2:i % 2 + 1], total[:, i % 2:i % 2 + 1]).then_inc(rec_ready, 1)

                    def maximum(i):
                        done = upto[i] + sum(n > 1 for n in chunks[:i])
                        for c in range(chunks[i]):
                            w = min(BLK, (i + 1) * P - c * BLK)
                            dve.wait_ge(s_ready, h * NC + (upto[i] + c + 1))
                            bank = ps[:, bank0(i) + c, :]
                            if c == chunks[i] - 1:
                                diag = bank[:, w - P:w]
                                dve.tensor_tensor(diag, diag, diag_neg[:, :], ALU.add).then_inc(neg_done, 1)
                                dve.wait_ge(neg_done, h * NT + (i + 1))
                            dve.tensor_reduce(mxc[:, c:c + 1], bank[:, 0:w], AX.X, ALU.max).then_inc(mx_step, 1)
                            done += 1
                        top = mxc[:, 0:1]
                        dve.wait_ge(mx_step, h * mx_per_head + done)
                        if chunks[i] > 1:
                            dve.tensor_reduce(m[:, :], mxc[:, 0:chunks[i]], AX.X, ALU.max).then_inc(mx_step, 1)
                            dve.wait_ge(mx_step, h * mx_per_head + done + 1)
                            top = m[:, :]
                        dve.tensor_scalar(negm[:, i % 2:i % 2 + 1], top, -scale, None, ALU.mult).then_inc(negm_ready, 1)

                    keys(0)
                    maximum(0)
                    keys(2)
                    for i in range(NT):
                        evac(i, 0)
                        if chunks[i] > 1:
                            evac(i, 1)
                        if i == 3:
                            keys(6)
                        invert(i)
                        if i + 1 < NT:
                            maximum(i + 1)
                        if i == 1:
                            keys(4)
                        for c in range(2, chunks[i]):
                            evac(i, c)

            @block.scalar
            def _(act):
                start_counts(act, exp_done, o_done)
                with act.Fori(0, BIG_HEADS) as h:
                    def queries(n):
                        act.wait_ge(pj_ready, START + h * NPJ + (n + 1))
                        act.activation(KQ[:, 1, (n // 2) * BLK:(n // 2 + 1) * BLK], ps[:, 3, :],
                                       ACT.Copy).then_inc(q_done, 1)

                    def out(i):
                        act.wait_ge(av_done, START + h * NC + upto[i + 1])
                        act.wait_ge(rec_ready, h * NT + (i + 1))
                        act.activation(O[:, i, bass.ds(h * P, P)], ps[:, O_BANK, 0:P], ACT.Copy,
                                       scale=rec[:, i % 2:i % 2 + 1]).then_inc(o_done, 1)

                    def exponentials(i):
                        w = (i + 1) * P
                        act.wait_ge(negm_ready, h * NT + (i + 1))
                        act.wait_ge(turned, START + h * NC + upto[max(i - 1, 0)])
                        banks = ps[:, bank0(i):bank0(i) + chunks[i], :].rearrange("p b n -> p (b n)")
                        act.activation(probs[:, i % 2, 0:w], banks[:, 0:w], ACT.Exp, bias=negm[:, i % 2:i % 2 + 1],
                                       scale=scale, accum_out=total[:, i % 2:i % 2 + 1]).then_inc(exp_done, 1)

                    queries(1)
                    exponentials(0)
                    queries(3)
                    for i in range(1, NT):
                        if i == 3:
                            queries(5)
                        if i == 4:
                            queries(7)
                        exponentials(i)
                        out(i - 1)
                    out(NT - 1)


def big_head_output_conv(core, tag, O, X, cT, dram):
    nc, ps = core.nc, core.psum
    with ExitStack() as st:
        sem = lambda n: core.sem(st, f"{tag}_{n}")
        sb = lambda n, s, dt=F32: core.sb(st, f"{tag}_{n}", s, dt)
        wo = sb("wo", [P, BIG_HEADS, P])
        gamma, beta, cw = sb("gamma", [P, 1]), sb("beta", [P, 1]), sb("cw", [P, 3])
        OTt = sb("OTt", [P, 2, BIG_HEADS, P])
        N = sb("N", [P, NT, P])
        hpad = sb("hpad", [P, T + 2])
        stats = (sb("stats", [P, NT, 6]), sb("mv", [P, NT, 2]), sb("veps", [P, NT]), sb("rstd", [P, NT]))
        half = sb("half", [P, NT])
        w_in, pad_set, turned, ot_a, ot_d, y_ready, y_read = (
            sem(n) for n in ("w_in", "pad_set", "turned", "ot_a", "ot_d", "y_ready", "y_read"))
        var_ready, rstd_ready, half_set, n_ready, n_turned, h_ready = (
            sem(n) for n in ("var_ready", "rstd_ready", "half_set", "n_ready", "n_turned", "h_ready"))
        loads = [(wo[:, :, :], dram["wo"]), (gamma[:, :], dram["gamma"]), (beta[:, :], dram["beta"]), (cw[:, :], dram["cw"])]
        with nc.Block() as block:
            @block.sync
            def _(sp):
                for dst, src in loads:
                    sp.dma_start(dst, src).then_inc(w_in, 16)

            @block.gpsimd
            def _(pool):
                pool.memset(hpad[:, 0:2], 0.0).then_inc(pad_set, 1)
                pool.wait_ge(pad_set, 1)
                pool.memset(half[:, :], -0.5).then_inc(half_set, 1)
                pool.wait_ge(half_set, 1)
                for n in range(2):
                    rsqrt_pool(pool, stats, half, var_ready, rstd_ready, n + 1)

            @block.tensor
            def _(pe):
                pe.wait_ge(w_in, 16 * len(loads))

                def turn(t):
                    if t >= 2:
                        pe.wait_ge(ot_d, t - 1)
                        pe.wait_ge(ot_a, t - 1)
                    for f in range(BIG_HEADS):
                        mm = pe.transpose(ps[:, 2 * (t % 2) + f // 4, (f % 4) * P:(f % 4 + 1) * P],
                                          O[:, t, f * P:(f + 1) * P], core.ident[:, :])
                    mm.then_inc(turned, 1)

                def out(t):
                    pe.wait_ge(ot_d, t + 1)
                    pe.wait_ge(ot_a, t + 1)
                    if t >= 2:
                        pe.wait_ge(y_read, t - 1)
                    for f in range(BIG_HEADS):
                        mm = pe.matmul(ps[:, 4 + t % 2, 0:P], OTt[:, t % 2, f, :], wo[:, f, :],
                                       start=(f == 0), stop=(f == BIG_HEADS - 1))
                    mm.then_inc(y_ready, 1)

                turn(0)
                for t in range(1, NT):
                    turn(t)
                    out(t - 1)
                out(NT - 1)
                pe.wait_ge(n_ready, 1)
                for g in range(NB):
                    for i in range(TPB):
                        mm = pe.transpose(ps[:, g, i * P:(i + 1) * P], N[:, g * TPB + i, :], core.ident[:, :])
                    mm.then_inc(n_turned, 1)

            @block.scalar
            def _(act):
                for t in range(NT):
                    act.wait_ge(turned, t + 1)
                    if t >= 2:
                        act.wait_ge(y_ready, t - 1)
                    act.activation(OTt[:, t % 2, 4:8, :].rearrange("p f n -> p (f n)"), ps[:, 2 * (t % 2) + 1, :],
                                   ACT.Copy).then_inc(ot_a, 1)

            @block.vector
            def _(dve):
                chain = Chain(dve, sem("chain"))

                def add(t):
                    dve.wait_ge(y_ready, t + 1)
                    dve.tensor_tensor(X[:, t, :], ps[:, 4 + t % 2, 0:P], X[:, t, :], ALU.add).then_inc(y_read, 1)
                for t in range(NT):
                    dve.wait_ge(turned, t + 1)
                    if t >= 2:
                        dve.wait_ge(y_ready, t - 1)
                    dve.tensor_copy(OTt[:, t % 2, 0:4, :].rearrange("p f n -> p (f n)"),
                                    ps[:, 2 * (t % 2), :]).then_inc(ot_d, 1)
                    if t >= 1:
                        add(t - 1)
                add(NT - 1)
                dve.wait_ge(y_read, NT)
                layer_norm(dve, chain, X, X, stats, (var_ready,), (rstd_ready, 1), range(NT))
                layer_norm(dve, chain, X, N, stats, (var_ready,), (rstd_ready, 2), range(NT))
                dve.sem_inc(n_ready, 1)
                dve.wait_ge(w_in, 16 * len(loads))
                for g in range(NB):
                    dve.wait_ge(n_turned, g + 1)
                    chain.link(dve.tensor_scalar(hpad[:, 2 + g * BLK:2 + (g + 1) * BLK], ps[:, g, :], gamma[:, 0:1],
                                                 beta[:, 0:1], ALU.mult, ALU.add))
                chain.settle()
                dve.wait_ge(pad_set, 1)
                chain.link(dve.tensor_scalar(cT[:, :], hpad[:, 0:T], cw[:, 0:1], None, ALU.mult))
                chain.settle()
                for k in (1, 2):
                    chain.link(dve.scalar_tensor_tensor(out=cT[:, :], in0=hpad[:, k:k + T], scalar=cw[:, k:k + 1],
                                                        in1=cT[:, :], op0=ALU.mult, op1=ALU.add))
                    chain.settle()


def final_norm(core, tag, X, XA, acc, out):
    nc = core.nc
    with ExitStack() as st:
        sem = lambda n: core.sem(st, f"{tag}_{n}")
        sb = lambda n, s, dt=F32: core.sb(st, f"{tag}_{n}", s, dt)
        stats = (sb("stats", [P, NT, 6]), sb("mv", [P, NT, 2]), sb("veps", [P, NT]), sb("rstd", [P, NT]))
        half = sb("half", [P, NT])
        var_ready, rstd_ready, half_set, done, stored = (
            sem(n) for n in ("var_ready", "rstd_ready", "half_set", "done", "stored"))
        with nc.Block() as block:
            @block.gpsimd
            def _(pool):
                pool.memset(half[:, :], -0.5).then_inc(half_set, 1)
                pool.wait_ge(half_set, 1)
                rsqrt_pool(pool, stats, half, var_ready, rstd_ready, 1)

            @block.vector
            def _(dve):
                chain = Chain(dve, sem("chain"))
                for other in (XA, X):
                    for g in range(NB):
                        mine = slice(g * TPB, (g + 1) * TPB)
                        chain.link(dve.tensor_tensor(acc[:, mine, :], acc[:, mine, :], other[:, mine, :], ALU.add))
                    chain.settle()
                layer_norm(dve, chain, acc, acc, stats, (var_ready,), (rstd_ready, 1), range(NT))
                dve.sem_inc(done, 1)

            @block.sync
            def _(sp):
                sp.wait_ge(done, 1)
                sp.dma_start(out.rearrange("(t p) c -> p t c", p=P), acc[:, :, :]).then_inc(stored, 16)
                sp.wait_ge(stored, 16)


def load_start(core, pairs):
    with ExitStack() as st:
        loaded = core.sem(st, "start_loaded")
        with core.nc.Block() as block:
            @block.sync
            def _(sp):
                for dst, src in pairs:
                    sp.dma_start(dst, src).then_inc(loaded, 16)
                sp.wait_ge(loaded, 16 * len(pairs))


def copy_tokens(core, tag, src, dst):
    with ExitStack() as st:
        copied = core.sem(st, f"{tag}_copied")
        with core.nc.Block() as block:
            @block.vector
            def _(dve):
                dve.tensor_copy(dst[:, :, :], src[:, :, :]).then_inc(copied, 1)


def small_attention(core, tag, src_T, OT, dram, table, causal, biased, scratch, diag_neg):
    with ExitStack() as st:
        KS = core.sb(st, f"{tag}_KS", [ROWS, HEADS, T], BF16)
        QS = core.sb(st, f"{tag}_QS", [ROWS, HEADS, T], BF16)
        V = core.sb(st, f"{tag}_V", [P, NT, HEADS, 2 * HD])
        small_head_projections(core, tag + "p", src_T, dram, KS, QS, V, biased, table, scratch)
        with ExitStack() as st2:
            sel = core.sb(st2, f"{tag}_sel", [P, 2, NPACK, P])
            small_head_attention(core, tag + "a", KS, QS, V, OT, sel, dram["sel"], diag_neg, causal)


def two_layers(nc, a, out):
    scratch = nc.dram_tensor("split_scratch", [2, HEADS, TERMS, HD, BLK], BF16, kind="Internal").ap()
    with ExitStack() as stack:
        core = Core(nc, stack)
        sb = lambda n, s, dt=F32: core.sb(stack, n, s, dt)
        core.ident = sb("ident", [P, P])
        X = sb("X", [P, NT, P])
        AT = sb("AT", [P, T])
        diag_neg = sb("diag_neg", [P, P])
        load_start(core, [(X[:, :, :], a["x"].rearrange("(t p) c -> p t c", p=P)), (AT[:, :], a["xT"]),
                          (core.ident[:, :], a["ident"]), (diag_neg[:, :], a["diag_neg"])])

        small_attention(core, "a0", AT, AT, {**{n: a["l0_" + n] for n in ("wq", "wqr", "wk", "wkr", "wv", "bq",
                        "bqr", "bk", "bkr", "bv")}, "sel": a["sel"]}, a["rope0"], False, True, scratch, diag_neg)
        core.recycle_semaphores()
        with ExitStack() as st:
            comb = core.sb(st, "comb0", [P, NT, 9])
            hT = core.sb(st, "h0T", [P, T])
            acc = core.sb(st, "acc0", [P, NT, P])
            project_norm_route(core, "r0", AT, X, hT, comb, {"wo": a["l0_wo"], "bo": a["l0_bo"], "gamma": a["l0_gamma"],
                               "beta": a["l0_beta"], "rw": a["l0_rw"], "rank": a["rank8"]}, 8, True, True, True)
            experts(core, "e0", hT, comb, acc, a["l0_gate_up"], a["l0_down"], 8, 3, (a["l0_sgu"], a["l0_sd"]))
            norm_l2_norm(core, "n0", X, acc, AT, {"gamma": a["l1_gamma"]})

        core.recycle_semaphores()
        with ExitStack() as st:
            O = core.sb(st, "O1", [P, NT, BIG_HEADS * BIG_HD])
            with ExitStack() as st2:
                V = core.sb(st2, "V1", [P, NT, BIG_HEADS * BIG_HD])
                big_head_values(core, "v1", AT, V, a["l1_big_wv"])
                big_head_attention(core, "b1", AT, V, O, a["l1_wqk"], diag_neg)
            big_head_output_conv(core, "o1", O, X, AT, {"wo": a["l1_wout"].rearrange("(f p) n -> p f n", p=P),
                                 "gamma": a["l1_ln1_w"], "beta": a["l1_ln1_b"], "cw": a["l1_conv"]})

        core.recycle_semaphores()
        small_attention(core, "a1", AT, AT, {**{n: a["l1_" + n] for n in ("wq", "wqr", "wk", "wkr", "wv")},
                        "sel": a["sel"]}, a["rope1"], True, False, scratch, diag_neg)
        with ExitStack() as st:
            XA = core.sb(st, "XA", [P, NT, P])
            comb = core.sb(st, "comb1", [P, NT, 4])
            hT = core.sb(st, "h1T", [P, T])
            acc = core.sb(st, "acc1", [P, NT, P])
            copy_tokens(core, "c1", X, XA)
            project_norm_route(core, "r1", AT, XA, hT, comb, {"wo": a["l1_proj"], "gamma": a["l1_ln2_w"],
                               "beta": a["l1_ln2_b"], "rw": a["l1_rw"], "rank": a["rank4"]}, 4, False, False, False)
            experts(core, "e1", hT, comb, acc, a["l1_gate_up"], a["l1_down"], 4, 4, None)
            final_norm(core, "f1", X, XA, acc, out)


def constants():
    import numpy as np
    f = np.float32
    c = {"ident": np.eye(P, dtype=f)}
    q, k = np.arange(P)[:, None], np.arange(P)[None, :]
    c["diag_neg"] = np.where(k > q, f(NEG), f(0)).astype(f)
    inv = (f(1.0) / np.power(f(10000.0), np.arange(0, HD, 2, dtype=f) / f(HD))).astype(f)
    ang = (np.arange(T, dtype=f)[:, None] * inv[None, :]).astype(f)
    sign = np.where(np.arange(HD) < HD // 2, f(-1), f(1))
    for name, col in (("rope0", np.arange(HD) // 2), ("rope1", np.arange(HD) % (HD // 2))):
        cos = np.cos(ang).astype(f)[:, col].T
        sin = (np.sin(ang).astype(f)[:, col] * sign[None, :]).T
        c[name] = np.ascontiguousarray(np.stack([np.tile(cos, (HEADS, 1)), np.tile(sin, (HEADS, 1))], 1), dtype=f)
    sel = np.zeros((P, 2, NPACK, P), f)
    for p in range(NPACK):
        for j in range(HPP):
            for d in range(HD):
                sel[32 * j + d, 0, p, (HPP * p + j) * HD + d] = 1
                sel[32 * j + HD + d, 1, p, (HPP * p + j) * HD + d] = 1
    c["sel"] = sel
    for e in (8, 4):
        c[f"rank{e}"] = np.broadcast_to(np.arange(e, 0, -1, dtype=f), (P, NT, e)).copy()
    return c


def layouts(i):
    import numpy as np
    t = lambda x: np.ascontiguousarray(np.asarray(x).T)
    col = lambda x: np.ascontiguousarray(np.asarray(x).reshape(P, 1))
    rows = lambda x: np.ascontiguousarray(np.broadcast_to(np.asarray(x).reshape(1, P), (P, P)))
    turn = np.arange(P) // HD * HD + (np.arange(P) % HD + HD // 2) % HD
    x = np.asarray(i["L0_attn_x"]).reshape(T, P)
    d = {"x": np.ascontiguousarray(x), "xT": t(x)}
    for n in "qkv":
        d[f"l0_w{n}"] = t(i[f"L0_attn_w{n}"])
    for n in "qk":
        d[f"l0_w{n}r"] = t(np.asarray(i[f"L0_attn_w{n}"])[turn])
        d[f"l0_b{n}"] = col(i[f"L0_attn_b{n}"])
        d[f"l0_b{n}r"] = col(np.asarray(i[f"L0_attn_b{n}"])[turn])
    d["l0_bv"], d["l0_bo"], d["l0_wo"] = rows(i["L0_attn_bv"]), rows(i["L0_attn_bo"]), t(i["L0_attn_wo"])
    d["l0_gamma"], d["l0_beta"], d["l0_rw"] = col(i["L0_ffn_ln_gamma"]), col(i["L0_ffn_ln_beta"]), t(i["L0_ffn_router_w"])
    d["l0_gate_up"] = np.ascontiguousarray(np.asarray(i["L0_ffn_gate_up_w"]).transpose(0, 2, 1))
    d["l0_down"] = np.ascontiguousarray(np.asarray(i["L0_ffn_down_w"]).transpose(0, 2, 1))
    d["l0_sgu"], d["l0_sd"] = t(i["L0_ffn_shared_gate_up_w"]), t(i["L0_ffn_shared_down_w"])
    d["l1_gamma"] = col(i["L1_attn_gamma"])
    w = np.asarray(i["L1_attn_w_qkv"]).reshape(3, BIG_HEADS, BIG_HD, P)
    d["l1_wqk"] = np.ascontiguousarray(w[:2].transpose(3, 1, 0, 2).reshape(P, -1))
    d["l1_big_wv"] = np.ascontiguousarray(w[2].transpose(2, 0, 1).reshape(P, -1))
    d["l1_wout"] = t(i["L1_attn_w_out"])
    for n in ("ln1_w", "ln1_b", "ln2_w", "ln2_b"):
        d["l1_" + n] = col(i["L1_ffn_" + n])
    d["l1_conv"] = np.ascontiguousarray(np.asarray(i["L1_ffn_conv_w"]).reshape(P, 3))
    aw = np.asarray(i["L1_ffn_attn_w"])
    for n, k in zip("qkv", range(3)):
        d[f"l1_w{n}"] = np.ascontiguousarray(aw[:, k * P:(k + 1) * P])
    for n, k in zip("qk", range(2)):
        d[f"l1_w{n}r"] = np.ascontiguousarray(aw[:, k * P:(k + 1) * P][:, turn])
    d["l1_proj"], d["l1_rw"] = np.ascontiguousarray(i["L1_ffn_proj_w"]), np.ascontiguousarray(i["L1_ffn_router_w"])
    d["l1_gate_up"], d["l1_down"] = np.ascontiguousarray(i["L1_ffn_expert_wv"]), np.ascontiguousarray(i["L1_ffn_expert_proj"])
    return d


def kernel(**inputs):
    import numpy as np
    import concourse.bacc as bacc
    from concourse.bass_utils import run_bass_kernel_spmd

    nc = bacc.Bacc("TRN2", target_bir_lowering=False, num_devices=1)
    arrays = {f"in_{n}": v for n, v in {**layouts(inputs), **constants()}.items()}
    aps = {n[3:]: nc.dram_tensor(n, v.shape, mybir.dt.from_np(v.dtype), kind="ExternalInput").ap()
           for n, v in arrays.items()}
    out = nc.dram_tensor("out_tokens", (T, P), F32, kind="ExternalOutput").ap()
    two_layers(nc, aps, out)
    r = run_bass_kernel_spmd(nc, [arrays], core_ids=[0])
    return np.asarray(r.results[0]["out_tokens"]).reshape(1, T, P)
```
